# Optimizing a Trainium2 kernel written in Bass

```python
import numpy as np
import jax
import jax.numpy as jnp

def _softmax(x, axis=-1):
    return jax.nn.softmax(x, axis=axis)

def _gelu(x):
    return jax.nn.gelu(x, approximate=True)

def _silu(x):
    return jax.nn.silu(x)

def _sigmoid(x):
    return jax.nn.sigmoid(x)

def _layernorm(x, axis=-1, eps=1e-05):
    m = jnp.mean(x, axis=axis, keepdims=True)
    v = jnp.var(x, axis=axis, keepdims=True)
    return (x - m) / jnp.sqrt(v + eps)

def _scatter_add(tgt, idx, src, axis=0):
    return tgt.at[idx].add(src)

def _segment_sum(src, seg, n):
    return jax.ops.segment_sum(src, seg, n)
kernel_name = 'mk_recurrent_d1_jaxref_r8_5a8500'

def setup_inputs(seed: int=0):
    np.random.seed(seed)
    _w = jnp.asarray

    def _L0_attn_setup():
        import jax, jax.numpy as jnp
        import numpy as np
        H = 16
        C = 128
        N = C // H
        Q = 32

        def _wkv_chunked(r, k, v, time_decay, time_faaaa):
            B, Hh, T, Nn = r.shape
            nc = T // Q
            wd = jnp.exp(-jnp.exp(time_decay))
            u = time_faaaa
            pw = wd[:, None] ** jnp.arange(Q, dtype=r.dtype)
            ws = wd ** Q
            wk = pw[:, ::-1]
            wb = pw
            ii = jnp.arange(Q)[:, None]
            jj = jnp.arange(Q)[None, :]
            Wmat = jnp.where(ii > jj, wd[:, None, None] ** jnp.maximum(ii - jj - 1, 0), jnp.where(ii == jj, u[:, None, None], 0.0))
            to_chunks = lambda a: a.reshape(B, Hh, nc, Q, Nn).transpose(2, 0, 1, 3, 4)
            rc, kc, vc = (to_chunks(r), to_chunks(k), to_chunks(v))

            def step(state, inp):
                rr, kk, vv = inp
                A = jnp.einsum('bhqn,bhpn->bhqp', rr, kk) * Wmat
                y = jnp.einsum('bhqp,bhpn->bhqn', A, vv) + jnp.einsum('bhqn,bhnm->bhqm', rr, state) * wb[None, :, :, None]
                new_state = ws[None, :, None, None] * state + jnp.einsum('bhqn,bhqm->bhnm', kk * wk[None, :, :, None], vv)
                return (new_state, y)
            state0 = jnp.zeros((B, Hh, Nn, Nn), dtype=r.dtype)
            state, ys = jax.lax.scan(step, state0, (rc, kc, vc))
            y = ys.transpose(1, 2, 0, 3, 4).reshape(B, Hh, T, Nn)
            return (y, state)

        def _reference_tuple_inner(x, time_maa_k, time_maa_v, time_maa_r, time_decay, time_faaaa, Wr, br, Wk, bk, Wv, bv, Wo, bo):
            B, T, Cc = x.shape
            xx = jnp.concatenate([jnp.zeros_like(x[:, :1]), x[:, :-1]], axis=1) - x
            xk = x + xx * time_maa_k
            xv = x + xx * time_maa_v
            xr = x + xx * time_maa_r
            proj = lambda a, W, b: a @ W.T + b
            split = lambda a: a.reshape(B, T, H, N).transpose(0, 2, 1, 3)
            r = split(proj(xr, Wr, br))
            k = split(proj(xk, Wk, bk))
            v = split(proj(xv, Wv, bv))
            y, state = _wkv_chunked(r, k, v, time_decay, time_faaaa)
            y = y.transpose(0, 2, 1, 3).reshape(B, T, Cc)
            out = proj(y, Wo, bo)
            return (out, state)
        key = jax.random.key(seed)
        ks = jax.random.split(key, 16)
        B, T = (4, 256)
        x = jax.random.normal(ks[0], (B, T, C), dtype=jnp.float32)
        ddd = jnp.arange(C, dtype=jnp.float32) / C
        time_maa_k = 1.0 - ddd
        time_maa_v = 1.0 - ddd
        time_maa_r = 1.0 - jnp.sqrt(ddd)
        h = jnp.arange(H, dtype=jnp.float32)
        time_decay = -6.0 + 5.0 * (h / (H - 1)) ** 0.7
        time_faaaa = jnp.zeros((H,), dtype=jnp.float32)
        s = 0.02
        Wr = jax.random.normal(ks[1], (C, C), dtype=jnp.float32) * s
        Wk = jax.random.normal(ks[2], (C, C), dtype=jnp.float32) * s
        Wv = jax.random.normal(ks[3], (C, C), dtype=jnp.float32) * s
        Wo = jax.random.normal(ks[4], (C, C), dtype=jnp.float32) * s
        br = jax.random.normal(ks[5], (C,), dtype=jnp.float32) * s
        bk = jax.random.normal(ks[6], (C,), dtype=jnp.float32) * s
        bv = jax.random.normal(ks[7], (C,), dtype=jnp.float32) * s
        bo = jax.random.normal(ks[8], (C,), dtype=jnp.float32) * s
        return dict(x=x, time_maa_k=time_maa_k, time_maa_v=time_maa_v, time_maa_r=time_maa_r, time_decay=time_decay, time_faaaa=time_faaaa, Wr=Wr, br=br, Wk=Wk, bk=bk, Wv=Wv, bv=bv, Wo=Wo, bo=bo)
    _L0_attn_in = _L0_attn_setup()

    def _L0_ffn_setup():
        import jax, jax.numpy as jnp
        import numpy as np
        B, S, D, F, E, NS, K = (2, 128, 128, 512, 8, 8, 2)
        FS = F // NS
        key = jax.random.key(seed)
        ks = jax.random.split(key, 8)
        scale = 0.02
        return {'hidden_states': jax.random.normal(ks[0], (B, S, D), jnp.float32), 'gate_W': jax.random.normal(ks[1], (E, D), jnp.float32) * scale, 'w1_e': jax.random.normal(ks[2], (E, D, F), jnp.float32) * scale, 'w3_e': jax.random.normal(ks[3], (E, D, F), jnp.float32) * scale, 'w2_e': jax.random.normal(ks[4], (E, F, D), jnp.float32) * scale, 'w1_s': jax.random.normal(ks[5], (NS, D, FS), jnp.float32) * scale, 'w3_s': jax.random.normal(ks[6], (NS, D, FS), jnp.float32) * scale, 'w2_s': jax.random.normal(ks[7], (NS, FS, D), jnp.float32) * scale}
    _L0_ffn_in = _L0_ffn_setup()
    _d = {'L0_attn_x': _L0_attn_in['x'], 'L0_attn_time_maa_k': _L0_attn_in['time_maa_k'], 'L0_attn_time_maa_v': _L0_attn_in['time_maa_v'], 'L0_attn_time_maa_r': _L0_attn_in['time_maa_r'], 'L0_attn_time_decay': _L0_attn_in['time_decay'], 'L0_attn_time_faaaa': _L0_attn_in['time_faaaa'], 'L0_attn_Wr': _L0_attn_in['Wr'], 'L0_attn_br': _L0_attn_in['br'], 'L0_attn_Wk': _L0_attn_in['Wk'], 'L0_attn_bk': _L0_attn_in['bk'], 'L0_attn_Wv': _L0_attn_in['Wv'], 'L0_attn_bv': _L0_attn_in['bv'], 'L0_attn_Wo': _L0_attn_in['Wo'], 'L0_attn_bo': _L0_attn_in['bo'], 'L0_ffn_gate_W': _L0_ffn_in['gate_W'], 'L0_ffn_w1_e': _L0_ffn_in['w1_e'], 'L0_ffn_w3_e': _L0_ffn_in['w3_e'], 'L0_ffn_w2_e': _L0_ffn_in['w2_e'], 'L0_ffn_w1_s': _L0_ffn_in['w1_s'], 'L0_ffn_w3_s': _L0_ffn_in['w3_s'], 'L0_ffn_w2_s': _L0_ffn_in['w2_s']}
    _x0 = _d['L0_attn_x']
    _d['L0_attn_x'] = jax.random.normal(jax.random.fold_in(jax.random.key(seed), 1), (16, 512, 128), dtype=_x0.dtype)
    del _x0
    return _d

def reference(L0_attn_x, L0_attn_time_maa_k, L0_attn_time_maa_v, L0_attn_time_maa_r, L0_attn_time_decay, L0_attn_time_faaaa, L0_attn_Wr, L0_attn_br, L0_attn_Wk, L0_attn_bk, L0_attn_Wv, L0_attn_bv, L0_attn_Wo, L0_attn_bo, L0_ffn_gate_W, L0_ffn_w1_e, L0_ffn_w3_e, L0_ffn_w2_e, L0_ffn_w1_s, L0_ffn_w3_s, L0_ffn_w2_s):

    def _L0_attn_ref(x, time_maa_k, time_maa_v, time_maa_r, time_decay, time_faaaa, Wr, br, Wk, bk, Wv, bv, Wo, bo):
        import jax, jax.numpy as jnp
        import numpy as np
        H = 16
        C = 128
        N = C // H
        Q = 32

        def _wkv_chunked(r, k, v, time_decay, time_faaaa):
            B, Hh, T, Nn = r.shape
            nc = T // Q
            wd = jnp.exp(-jnp.exp(time_decay))
            u = time_faaaa
            pw = wd[:, None] ** jnp.arange(Q, dtype=r.dtype)
            ws = wd ** Q
            wk = pw[:, ::-1]
            wb = pw
            ii = jnp.arange(Q)[:, None]
            jj = jnp.arange(Q)[None, :]
            Wmat = jnp.where(ii > jj, wd[:, None, None] ** jnp.maximum(ii - jj - 1, 0), jnp.where(ii == jj, u[:, None, None], 0.0))
            to_chunks = lambda a: a.reshape(B, Hh, nc, Q, Nn).transpose(2, 0, 1, 3, 4)
            rc, kc, vc = (to_chunks(r), to_chunks(k), to_chunks(v))

            def step(state, inp):
                rr, kk, vv = inp
                A = jnp.einsum('bhqn,bhpn->bhqp', rr, kk) * Wmat
                y = jnp.einsum('bhqp,bhpn->bhqn', A, vv) + jnp.einsum('bhqn,bhnm->bhqm', rr, state) * wb[None, :, :, None]
                new_state = ws[None, :, None, None] * state + jnp.einsum('bhqn,bhqm->bhnm', kk * wk[None, :, :, None], vv)
                return (new_state, y)
            state0 = jnp.zeros((B, Hh, Nn, Nn), dtype=r.dtype)
            state, ys = jax.lax.scan(step, state0, (rc, kc, vc))
            y = ys.transpose(1, 2, 0, 3, 4).reshape(B, Hh, T, Nn)
            return (y, state)

        def _reference_tuple_inner(x, time_maa_k, time_maa_v, time_maa_r, time_decay, time_faaaa, Wr, br, Wk, bk, Wv, bv, Wo, bo):
            B, T, Cc = x.shape
            xx = jnp.concatenate([jnp.zeros_like(x[:, :1]), x[:, :-1]], axis=1) - x
            xk = x + xx * time_maa_k
            xv = x + xx * time_maa_v
            xr = x + xx * time_maa_r
            proj = lambda a, W, b: a @ W.T + b
            split = lambda a: a.reshape(B, T, H, N).transpose(0, 2, 1, 3)
            r = split(proj(xr, Wr, br))
            k = split(proj(xk, Wk, bk))
            v = split(proj(xv, Wv, bv))
            y, state = _wkv_chunked(r, k, v, time_decay, time_faaaa)
            y = y.transpose(0, 2, 1, 3).reshape(B, T, Cc)
            out = proj(y, Wo, bo)
            return (out, state)
        return _reference_tuple_inner(x, time_maa_k, time_maa_v, time_maa_r, time_decay, time_faaaa, Wr, br, Wk, bk, Wv, bv, Wo, bo)[0]

    def _L0_ffn_ref(hidden_states, gate_W, w1_e, w3_e, w2_e, w1_s, w3_s, w2_s):
        import jax, jax.numpy as jnp
        import numpy as np
        B, S, D, F, E, NS, K = (2, 128, 128, 512, 8, 8, 2)
        FS = F // NS
        b, s, d = hidden_states.shape
        e = gate_W.shape[0]
        flat = hidden_states.reshape(-1, d)
        T = flat.shape[0]
        logits = (flat @ gate_W.T).astype(jnp.float32)
        probs = jax.nn.softmax(logits, axis=-1)
        top_v, top_i = jax.lax.top_k(probs, K)
        gates = jnp.zeros((T, e), probs.dtype).at[jnp.arange(T)[:, None], top_i].set(top_v)
        g = jax.nn.silu(jnp.einsum('td,edf->etf', flat, w1_e))
        u = jnp.einsum('td,edf->etf', flat, w3_e)
        out_e = jnp.einsum('etf,efd->etd', g * u, w2_e)
        routed = jnp.einsum('te,etd->td', gates, out_e).reshape(b, s, d)
        gs = jax.nn.silu(jnp.einsum('bsd,ndf->nbsf', hidden_states, w1_s))
        us = jnp.einsum('bsd,ndf->nbsf', hidden_states, w3_s)
        shared = jnp.einsum('nbsf,nfd->bsd', gs * us, w2_s) / w1_s.shape[0]
        alpha = 0.5
        return alpha * shared + (1.0 - alpha) * routed
    x = L0_attn_x
    xn = _layernorm(x, axis=-1)
    s = _L0_attn_ref(xn, L0_attn_time_maa_k, L0_attn_time_maa_v, L0_attn_time_maa_r, L0_attn_time_decay, L0_attn_time_faaaa, L0_attn_Wr, L0_attn_br, L0_attn_Wk, L0_attn_bk, L0_attn_Wv, L0_attn_bv, L0_attn_Wo, L0_attn_bo)
    g = _silu(_L0_ffn_ref(xn, L0_ffn_gate_W, L0_ffn_w1_e, L0_ffn_w3_e, L0_ffn_w2_e, L0_ffn_w1_s, L0_ffn_w3_s, L0_ffn_w2_s))
    x = x + s * g
    return x

_drawn_inputs = setup_inputs


def setup_inputs(seed=0):
    import zlib

    import numpy as np

    out = dict(_drawn_inputs(seed))
    spreads = {'L0_attn_time_faaaa': (0.0, 0.1)}
    factors = {}
    for name, (base, spread) in spreads.items():
        noise = np.random.default_rng([zlib.crc32(name.encode()), seed]).standard_normal(out[name].shape)
        drawn = base * np.exp(spread * noise) if base else spread * noise
        out[name] = jnp.asarray(drawn.astype(out[name].dtype))
    for name, factor in factors.items():
        out[name] = (out[name] * factor).astype(out[name].dtype)
    return out
```

```python
from contextlib import ExitStack

import numpy as np
import concourse.bass as bass
from concourse import mybir

F32, F16, I32 = mybir.dt.float32, mybir.dt.float16, mybir.dt.int32
ALU = mybir.AluOpType
ACT = mybir.ActivationFunctionType
AX = mybir.AxisListType.X

P = 128
HEADS, HD = 16, 8
Q = 32
CH = P // Q
HPG = Q // HD
SEQ = 512
TPS = SEQ // P
EXPERTS, WIDTH = 8, 512
FC = WIDTH // P
EW = 3 * WIDTH
UNIT = 256
XS = SEQ + 2

SW = 2.0 ** 8
SA = 2.0 ** 8
SS = 2.0 ** 4
SY = 2.0 ** 6

CONST = {}


def constants(routed):
    p = np.arange(P)
    j, i = p % Q, np.arange(Q)
    parts = {
        "ident": np.eye(P),
        "before": p[:, None] < p[None, :],
        "head": (p[:, None] // HD == p[None, :] // HD) * (SS / SW / SW),
        "first2": np.repeat(p[:, None] < 2, P, 1),
        "first2y": np.repeat(p[:, None] < 2, P, 1) * SY,
        "slot": (p[:, None] // HD) % HPG == np.arange(HPG)[None, :],
        "slot_y": ((p[:, None] // HD) % HPG == np.arange(HPG)[None, :]) * (SY / SA / SW),
        "gap": np.maximum(i[None, :] - j[:, None] - 1, 0),
        "later": (i[None, :] > j[:, None]) * (SA / SW / SW),
        "same": (i[None, :] == j[:, None]) * (SA / SW / SW),
        "step": np.repeat(i[None, :], P, 0),
        "to_end": -(Q - 1 - j[:, None]),
        "rank": np.repeat(EXPERTS - np.arange(EXPERTS)[None, :], P, 0),
        "units": np.repeat(UNIT * np.arange(routed)[None, :], P, 0),
        "ones": np.ones((P, 1)),
    }
    at, out = 0, []
    for name, a in parts.items():
        a = np.asarray(a, np.float32)
        CONST[name] = (at, a.shape[1])
        at += a.shape[1]
        out.append(a)
    return np.concatenate(out, 1)


def build(nc, nb, x, decay, per_head, maa, wT, bias, bias_rows, gateT, w1e, w3e, w2e, w1s, w3s, w2s, const, out):
    NTOK = nb * SEQ
    NT = NTOK // P
    SHARED = NTOK // UNIT
    ROUTED = 2 * NTOK // UNIT + EXPERTS - 1
    NU = SHARED + ROUTED
    NG = nb // 4
    NA = TPS * NG
    TPU = UNIT // P
    NTHR = NTOK // UNIT

    rows_in = nc.dram_tensor("sorted_rows", (ROUTED * UNIT, P), F32, kind="Internal").ap()
    rows_out = nc.dram_tensor("sorted_results", (ROUTED * UNIT, P), F32, kind="Internal").ap()

    ctx = ExitStack()
    with ctx:
        def sb(name, shape, dt=F32):
            return ctx.enter_context(nc.sbuf_tensor(name, shape, dt))

        def carve(*regions):
            left = [[r, 0] for r in regions]

            def take(shape, dt=F32):
                n = int(np.prod(shape[1:]))
                words = n if dt != F16 else n // 2
                for r in left:
                    if r[1] + words <= r[0].shape[1]:
                        v = r[0][:, r[1]:r[1] + words]
                        r[1] += words
                        break
                else:
                    raise ValueError("no room")
                if dt != F32:
                    v = v.bitcast(dt)
                names = "abc"[:len(shape) - 1]
                if len(names) > 1:
                    v = v.rearrange(f"p ({' '.join(names)}) -> p {' '.join(names)}", **dict(zip(names, shape[1:])))
                return v
            return take

        sems, waited = {}, {}

        def sem(name):
            if name not in sems:
                sems[name] = ctx.enter_context(nc.semaphore(name))
            return sems[name]

        def done(instruction, name, n=1):
            instruction.then_inc(sem(name), n)

        def wait(eng, name, n):
            key = (str(eng.engine), name)
            if n > waited.get(key, 0):
                waited[key] = n
                eng.wait_ge(sem(name), n)

        cst = sb("cst", [P, const.shape[1]])

        def C(name):
            at, n = CONST[name]
            return cst[:, at:at + n]

        rows = sb("rows", [P, NT, P])
        xh = sb("xh", [P, nb * XS], F16)
        xl = sb("xl", [P, nb * XS], F16)
        wwords = sb("wwords", [P, (EXPERTS + 1) * EW])
        wh = wwords[:, 0:wwords.shape[1] // 2].bitcast(F16)
        wl = wwords[:, wwords.shape[1] // 2:].bitcast(F16)
        stage = sb("stage", [P, 2, EW])
        ffn = sb("ffn", [P, NT, P])

        before = sb("before", [P, P], F16)
        ones16 = sb("ones16", [P, P], F16)
        stats = sb("stats", [P, NT, 6])
        mv = sb("mv", [P, NT, 2])
        vare = sb("vare", [P, NT])
        std = sb("std", [P, NT])
        rstd = sb("rstd", [P, NT])
        gate32 = sb("gate32", [P, EXPERTS])
        gateh = sb("gateh", [P, EXPERTS], F16)
        gatel = sb("gatel", [P, EXPERTS], F16)

        psum = [ctx.enter_context(nc.psum_tensor(f"bank{i}", [P, 512], F32)) for i in range(8)]

        NXB = 3
        srows = sb("srows", [P, NXB, TPU, P])
        sxh = sb("sxh", [P, NXB, UNIT], F16)
        sxl = sb("sxl", [P, NXB, UNIT], F16)
        hidden = sb("hidden", [P, 8 * 2 * UNIT])
        take = carve(hidden[:, :])
        sg = take([P, 2, 2 * UNIT])
        gu = take([P, 2, 2 * UNIT])
        guh = take([P, 2, FC * UNIT], F16)
        gul = take([P, 2, FC * UNIT], F16)
        NYB = 3
        ybuf = sb("ybuf", [P, NYB, TPU, P])

        take = carve(ffn[:, NT // 2:, :].rearrange("p a b -> p (a b)"))
        lg = take([P, NT, EXPERTS])
        ta = take([P, NT, EXPERTS])
        tb = take([P, NT, EXPERTS])
        oh = [take([P, NT, EXPERTS]) for k in range(2)]
        chosen = take([P, NT, EXPERTS], F16)
        top = [sb(f"top{k}", [P, NT]) for k in range(2)]
        tc_ = sb("tc_", [P, NT])
        zsum = sb("zsum", [P, NT])
        gates = [sb(f"gates{k}", [P, NT]) for k in range(2)]
        incl = take([P, EXPERTS, NT])
        posn = take([P, NT, EXPERTS])
        posf = sb("posf", [P, NT])
        pos = [sb(f"pos{k}", [P, NT], I32) for k in range(2)]
        early = carve(hidden[:, :])
        over = early([P, EXPERTS, NTHR])
        room = sb("room", [P, EXPERTS])
        ends = sb("ends", [P, EXPERTS])
        begins = sb("begins", [P, EXPERTS])
        eun = early([P, ROUTED, EXPERTS])
        eidf = sb("eidf", [P, ROUTED])
        eid = sb("eid", [P, ROUTED], I32)

        dec = sb("dec", [P, 1])
        hdc = sb("hdc", [P, 2 * HEADS])
        rate = sb("rate", [P, 1])
        nrate = sb("nrate", [P, 1])
        rates = sb("rates", [P, HEADS])
        wmat = sb("wmat", [P, HEADS, Q])
        wtmp = early([P, HEADS, Q])
        wk = sb("wk", [P, P])
        wb0 = early([P, Q])
        wb = sb("wb", [P, Q])
        ws = sb("ws", [P, 1])
        mx = sb("mx", [P, 3])
        omx = sb("omx", [P, 3])
        w32 = early([P, 4, P])
        ws32 = early([P, 7, P])
        wph = sb("wph", [P, 7, P], F16)
        wpl = sb("wpl", [P, 7, P], F16)
        brk = sb("brk", [P, 2])
        brs = sb("brs", [P, 2])
        bro = early([P, 3 * P])
        brh = early([P, 3 * P], F16)
        brl = early([P, 3 * P], F16)
        brw = sb("brw", [P, 3 * P], F16)
        f2 = sb("f2", [P, P], F16)
        f2y = sb("f2y", [P, P], F16)
        slot16 = sb("slot16", [P, HPG])

        take = carve(wwords[:, :], hidden[:, :], rows[:, :, :].rearrange("p a b -> p (a b)"),
                     stage[:, :, :].rearrange("p a b -> p (a b)"))
        rh = take([P, 2, 512], F16)
        rl = take([P, 2, 512], F16)
        rmh = take([P, 2, HPG, 512], F16)
        rml = take([P, 2, HPG, 512], F16)
        kh = take([P, 2, 512], F16)
        kl = take([P, 2, 512], F16)
        kt = take([P, 2, 2, P])
        kth = take([P, 2, 4, P], F16)
        ktl = take([P, 2, 4, P], F16)
        vh = take([P, 2, 4, P], F16)
        vl = take([P, 2, 4, P], F16)
        a32 = take([P, 2, 512])
        ah = take([P, 2, 512], F16)
        al = take([P, 2, 512], F16)
        um = take([P, 2, 512])
        st = take([P, NG, 512])
        sh = take([P, NG, 512], F16)
        sl = take([P, NG, 512], F16)
        yacc = take([P, 2, 4, P])
        yint = take([P, 2, 512])
        y32 = take([P, 2, 512])
        yh = take([P, 2, 512], F16)
        yl = take([P, 2, 512], F16)
        picked = [take([P, 2, 4, P]) for k in range(2)]
        xin = take([P, 2, 4, P])
        mo = take([P, 2, 4, P])
        gt = take([P, 2, 512])
        res = take([P, 2, 512])

        x_rows = x.rearrange("b (t p) d -> b p t d", p=P)
        x_unit = x.rearrange("(g b) (t p) d -> g t p b d", b=4, p=P)
        out_unit = out.rearrange("(g b) (t p) d -> g t p b d", b=4, p=P)

        block = ctx.enter_context(nc.Block())
        pe, act, dve, pool, sp = {}, {}, {}, {}, {}
        V, A, T, G = nc.vector, nc.scalar, nc.tensor, nc.gpsimd

        def rep(ap, n):
            return ap.unsqueeze(2).to_broadcast([ap.shape[0], ap.shape[1], n])

        def rep_mid(ap, n):
            return ap.unsqueeze(1).to_broadcast([ap.shape[0], n, ap.shape[1]])

        def sp_start():
            for b in range(nb):
                done(nc.sync.dma_start(rows[:, b * TPS:(b + 1) * TPS, :], x_rows[b]), f"x_in{b}", 16)
                if b == 0:
                    done(nc.sync.dma_start(cst[:, :], const), "const_in", 16)
                    done(nc.sync.dma_start(gate32[:, :], gateT), "gate_in", 16)
                    for dst, src in ((dec, decay), (hdc, per_head), (mx, maa), (w32, wT), (brk, bias)):
                        done(nc.sync.dma_start(dst[:], src), "small_in", 16)

        def sp_weights(e):
            s = e % 2
            if e >= 2:
                wait(nc.sync, "w_lo", e - 1)
            w1, w3, w2 = (w1s, w3s, w2s) if e == EXPERTS else (w1e[e], w3e[e], w2e[e])
            for i, w in enumerate((w1, w3, w2)):
                dst = stage[:, s, i * WIDTH:(i + 1) * WIDTH]
                if e == EXPERTS and i < 2:
                    w = w.rearrange("n d f -> d n f")
                    dst = dst.rearrange("p (n f) -> p n f", n=8)
                elif i == 2:
                    w = (w.rearrange("n f d -> (n f) d") if e == EXPERTS else w).rearrange("(c p) d -> p c d", p=P)
                    dst = dst.rearrange("p (c d) -> p c d", d=P)
                done(nc.sync.dma_start(dst, w), f"w_in{s}", 16)

        def act_zero():
            wait(A, "zeros", 1)
            n = ROUTED * UNIT
            z = zero_rows
            flat = rows_in.rearrange("(p a) d -> p (a d)", p=P)
            width, at = flat.shape[1], 0
            while at < width:
                k = min(z.shape[1], width - at)
                done(A.dma_start(flat[:, at:at + k], z[:, 0:k]), "zeroed", 16)
                at += k

        zero_rows = ffn[:, 0:NT // 2, :].rearrange("p a b -> p (a b)")
        zero_dmas = -(-ROUTED * UNIT // (NT // 2 * P))

        def dve_prologue():
            done(V.memset(ffn[:, 0:NT // 2, :], 0.0), "zeros")
            wait(V, "const_in", 16)
            done(V.tensor_copy(before[:, :], C("before")), "tri")
            done(V.memset(ones16[:, :], 1.0), "tri")
            wait(V, "gate_in", 16)
            done(V.tensor_scalar(gate32[:, :], gate32[:, :], SW, None, ALU.mult), "gate_s")
            wait(V, "gate_s", 1)
            done(V.tensor_copy(gateh[:, :], gate32[:, :]), "gate_s")
            wait(V, "gate_s", 2)
            done(V.tensor_tensor(gatel[:, :], gate32[:, :], gateh[:, :], ALU.subtract), "gate_s")

        def pool_prologue():
            for t in (xh, xl):
                for b in range(nb):
                    done(G.memset(t[:, b * XS:b * XS + 2], 0.0), "zero_cols")

        def dve_stats(b):
            wait(V, f"x_in{b}", 16)
            for t in range(b * TPS, (b + 1) * TPS):
                done(V.bn_stats(stats[:, t, :], rows[:, t, :]), "bn")
            wait(V, "bn", (b + 1) * TPS)
            for t in range(b * TPS, (b + 1) * TPS):
                done(V.bn_aggr(mv[:, t, :], stats[:, t, :]), "mv")
            wait(V, "mv", (b + 1) * TPS)
            done(V.tensor_scalar(vare[:, b * TPS:(b + 1) * TPS], mv[:, b * TPS:(b + 1) * TPS, 1], 1e-5, None,
                                 ALU.add), "vare")

        def act_std(b):
            wait(A, "vare", b + 1)
            done(A.activation(std[:, b * TPS:(b + 1) * TPS], vare[:, b * TPS:(b + 1) * TPS], ACT.Sqrt), "std")

        def dve_norm(b):
            wait(V, "std", b + 1)
            done(V.reciprocal(rstd[:, b * TPS:(b + 1) * TPS], std[:, b * TPS:(b + 1) * TPS]), "rstd")
            wait(V, "rstd", b + 1)
            for t in range(b * TPS, (b + 1) * TPS):
                done(V.tensor_scalar(rows[:, t, :], rows[:, t, :], mv[:, t, 0:1], rstd[:, t:t + 1],
                                     ALU.subtract, ALU.mult), "normed")

        def pe_flip(b):
            wait(T, "const_in", 16)
            wait(T, "normed", (b + 1) * TPS)
            if b >= 4:
                wait(T, "x_lo", b - 3)
            for t in range(TPS):
                i = T.transpose(psum[b % 4][:, t * P:(t + 1) * P], rows[:, b * TPS + t, :], C("ident"))
            done(i, "flipped")

        def act_flip(b):
            wait(A, "flipped", b + 1)
            done(A.copy(xh[:, b * XS + 2:(b + 1) * XS], psum[b % 4][:, :]), "x_hi")

        def dve_flip(b):
            wait(V, "x_hi", b + 1)
            done(V.tensor_tensor(xl[:, b * XS + 2:(b + 1) * XS], psum[b % 4][:, :], xh[:, b * XS + 2:(b + 1) * XS],
                                 ALU.subtract), "x_lo")

        def pe_gate(b):
            wait(T, "gate_s", 3)
            wait(T, "x_lo", b + 1)
            for t in range(TPS):
                at = b * XS + 2 + t * P
                o = psum[7][:, (b * TPS + t) * EXPERTS:(b * TPS + t + 1) * EXPERTS]
                T.matmul(o, xh[:, at:at + P], gateh[:, :], start=True, stop=False)
                T.matmul(o, xh[:, at:at + P], gatel[:, :], start=False, stop=False)
                i = T.matmul(o, xl[:, at:at + P], gateh[:, :], start=False, stop=True)
            done(i, "logits")

        def act_split_w(e):
            s = e % 2
            wait(A, f"w_in{s}", 48 * (e // 2 + 1))
            done(A.mul(wh[:, e * EW:(e + 1) * EW], stage[:, s, :], SW), "w_hi")

        def dve_split_w(e):
            wait(V, "w_hi", e + 1)
            wait(V, f"w_in{e % 2}", 48 * (e // 2 + 1))
            done(V.scalar_tensor_tensor(wl[:, e * EW:(e + 1) * EW], stage[:, e % 2, :], SW,
                                        wh[:, e * EW:(e + 1) * EW], ALU.mult, ALU.subtract), "w_lo")

        def dve_route():
            n = [0]

            def link(i):
                n[0] += 1
                done(i, "route")
                wait(V, "route", n[0])

            rank = C("rank").unsqueeze(1).to_broadcast([P, NT, EXPERTS])
            wait(V, "logits", nb)
            link(V.tensor_copy(lg[:, :, :], psum[7][:, 0:NT * EXPERTS].rearrange("p (t e) -> p t e", e=EXPERTS)))
            cur = lg
            for k in range(2):
                link(V.tensor_reduce(top[k][:, :], cur[:, :, :], AX, ALU.max))
                link(V.tensor_tensor(ta[:, :, :], cur[:, :, :], rep(top[k][:, :], EXPERTS), ALU.is_equal))
                link(V.tensor_tensor(ta[:, :, :], ta[:, :, :], rank, ALU.mult))
                link(V.tensor_reduce(tc_[:, :], ta[:, :, :], AX, ALU.max))
                link(V.tensor_tensor(oh[k][:, :, :], rep(tc_[:, :], EXPERTS), rank, ALU.is_equal))
                if k == 0:
                    link(V.scalar_tensor_tensor(tb[:, :, :], oh[0][:, :, :], -3e38, lg[:, :, :], ALU.mult, ALU.add))
                    cur = tb
            link(V.tensor_tensor(chosen[:, :, :], oh[0][:, :, :], oh[1][:, :, :], ALU.add))
            done(V.tensor_tensor(ta[:, :, :], lg[:, :, :], rep(top[0][:, :], EXPERTS), ALU.subtract), "shifted")
            done(V.tensor_tensor(tc_[:, :], top[1][:, :], top[0][:, :], ALU.subtract), "shifted")
            wait(V, "counts", 1)
            for e in range(EXPERTS):
                i = V.tensor_tensor_scan(
                    incl[:, e, :], C("ones").to_broadcast([P, NT]),
                    psum[1][:, 0:NT * EXPERTS].rearrange("p (t e) -> p e t", e=EXPERTS)[:, e, :],
                    0.0, ALU.mult, ALU.add)
                done(i, "scanned")
            wait(V, "scanned", EXPERTS)
            link(V.tensor_tensor(over[:, :, :], rep(incl[:, :, NT - 1], NTHR),
                                 rep_mid(C("units")[:, 0:NTHR], EXPERTS), ALU.is_gt))
            link(V.tensor_reduce(room[:, :], over[:, :, :], AX, ALU.add))
            link(V.tensor_scalar(room[:, :], room[:, :], float(UNIT), None, ALU.mult))
            link(V.tensor_tensor_scan(ends[:, :], C("ones").to_broadcast([P, EXPERTS]), room[:, :], 0.0,
                                      ALU.mult, ALU.add))
            link(V.tensor_tensor(begins[:, :], ends[:, :], room[:, :], ALU.subtract))
            link(V.tensor_tensor(eun[:, :, 1:EXPERTS], rep(C("units")[:, 0:ROUTED], EXPERTS - 1),
                                 rep_mid(begins[:, 1:EXPERTS], ROUTED), ALU.is_ge))
            link(V.tensor_reduce(eidf[:, :], eun[:, :, 1:EXPERTS], AX, ALU.add))
            done(V.tensor_copy(eid[:, :], eidf[:, :]), "unit_experts")
            tot = psum[1][:, 0:NT * EXPERTS].rearrange("p (t e) -> p t e", e=EXPERTS)
            cum = psum[0][:, 0:NT * EXPERTS].rearrange("p (t e) -> p t e", e=EXPERTS)
            link(V.tensor_tensor(posn[:, :, :], incl[:, :, :].rearrange("p e t -> p t e"), tot, ALU.subtract))
            link(V.tensor_tensor(posn[:, :, :], posn[:, :, :], cum, ALU.add))
            link(V.tensor_tensor(posn[:, :, :], posn[:, :, :], rep_mid(begins[:, :], NT), ALU.add))
            for k in range(2):
                link(V.tensor_tensor(tb[:, :, :], posn[:, :, :], oh[k][:, :, :], ALU.mult))
                link(V.tensor_reduce(posf[:, :], tb[:, :, :], AX, ALU.add))
                done(V.tensor_copy(pos[k][:, :], posf[:, :]), "places")
                wait(V, "places", k + 1)
            wait(V, "exps", 2)
            link(V.tensor_reduce(zsum[:, :], ta[:, :, :], AX, ALU.add))
            link(V.reciprocal(zsum[:, :], zsum[:, :]))
            done(V.tensor_scalar(gates[0][:, :], zsum[:, :], 0.5, None, ALU.mult), "gates")
            wait(V, "gates", 1)
            done(V.tensor_tensor(gates[1][:, :], tc_[:, :], gates[0][:, :], ALU.mult), "gates")

        def act_route():
            wait(A, "shifted", 2)
            done(A.activation(ta[:, :, :], ta[:, :, :], ACT.Exp, scale=1.0 / SW), "exps")
            done(A.activation(tc_[:, :], tc_[:, :], ACT.Exp, scale=1.0 / SW), "exps")

        ROUTE_CHOSEN = 1 + 5 * 2 + 1 + 1

        def pe_route():
            wait(T, "tri", 2)
            wait(T, "route", ROUTE_CHOSEN)
            m = chosen[:, :, :].rearrange("p t e -> p (t e)")
            T.matmul(psum[0][:, 0:NT * EXPERTS], before[:, :], m, start=True, stop=True)
            done(T.matmul(psum[1][:, 0:NT * EXPERTS], ones16[:, :], m, start=True, stop=True), "counts")

        def pool_scatter():
            wait(G, "places", 2)
            wait(G, "normed", NT)
            wait(G, "zeroed", 16 * zero_dmas)
            for t in range(NT):
                for k in range(2):
                    done(G.indirect_dma_start(rows_in, bass.IndirectOffsetOnAxis(pos[k][:, t:t + 1], 0),
                                              rows[:, t, :], None), "scattered", 16)

        def routed(v):
            return v >= SHARED

        def sp_sorted(v):
            r = v - SHARED
            wait(nc.sync, "scattered", 16 * 2 * NT)
            if r >= NXB:
                wait(nc.sync, "s_flipped", r - NXB + 1)
            done(nc.sync.dma_start(srows[:, r % NXB, :, :],
                                   rows_in[r * UNIT:(r + 1) * UNIT, :].rearrange("(t p) d -> p t d", p=P)),
                 f"s_in{r % NXB}", 16)

        def pe_sorted(v):
            r = v - SHARED
            wait(T, f"s_in{r % NXB}", 16 * (r // NXB + 1))
            if r == 0:
                wait(T, "route", ROUTE_CHOSEN)
            if r >= 2:
                wait(T, "s_lo", r - 1)
            for t in range(TPU):
                i = T.transpose(psum[6 + r % 2][:, t * P:(t + 1) * P], srows[:, r % NXB, t, :], C("ident"))
            done(i, "s_flipped")

        def act_sorted(v):
            r = v - SHARED
            wait(A, "s_flipped", r + 1)
            if r >= NXB:
                wait(A, "up", 2 * (v - NXB + 1))
            done(A.copy(sxh[:, r % NXB, :], psum[6 + r % 2][:, 0:UNIT]), "s_hi")

        def dve_sorted(v):
            r = v - SHARED
            wait(V, "s_hi", r + 1)
            done(V.tensor_tensor(sxl[:, r % NXB, :], psum[6 + r % 2][:, 0:UNIT], sxh[:, r % NXB, :],
                                 ALU.subtract), "s_lo")

        expert_at = {}

        def weights(v, part, c):
            at = part * WIDTH + c * P
            if not routed(v):
                at += EXPERTS * EW
                return wh[:, at:at + P], wl[:, at:at + P]
            d = bass.ds(expert_at[v] + at, P)
            return wh[:, d], wl[:, d]

        def pe_up(v, h):
            i = 2 * v + h
            if v == 0:
                wait(T, "w_lo", EXPERTS + 1)
                wait(T, "places", 2)
            if routed(v):
                if h == 0:
                    wait(T, "unit_experts", 1)
                    expert_at[v] = T.value_load(eid[0:1, v - SHARED:v - SHARED + 1], min_val=0,
                                                max_val=EXPERTS - 1) * EW
                r = v - SHARED
                wait(T, "s_lo", r + 1)
                mh, ml = sxh[:, r % NXB, :], sxl[:, r % NXB, :]
            else:
                at = v * UNIT // SEQ * XS + 2 + v * UNIT % SEQ
                mh, ml = xh[:, at:at + UNIT], xl[:, at:at + UNIT]
            if i >= 2:
                wait(T, "gated", i - 1)
            for part in range(2):
                for c in range(2):
                    a, b = weights(v, part, 2 * h + c)
                    o = psum[2 * (i % 2) + part][:, c * UNIT:(c + 1) * UNIT]
                    T.matmul(o, a, mh, start=True, stop=False)
                    T.matmul(o, a, ml, start=False, stop=False)
                    k = T.matmul(o, b, mh, start=False, stop=True)
            done(k, "up")

        def act_up(v, h):
            i = 2 * v + h
            wait(A, "up", i + 1)
            if i == 0:
                wait(A, "aconst_ready", 1)
            if i >= 2:
                wait(A, "gated", i - 1)
            done(A.activation(sg[:, i % 2, :], psum[2 * (i % 2)][:, :], ACT.Silu, scale=1.0 / SW), "silu")

        def dve_up(v, h):
            i = 2 * v + h
            wait(V, "silu", i + 1)
            if i >= 2:
                wait(V, "gu_lo", i - 1)
            done(V.tensor_tensor(gu[:, i % 2, :], sg[:, i % 2, :], psum[2 * (i % 2) + 1][:, :], ALU.mult), "gated")

        def act_split(v, h):
            i = 2 * v + h
            wait(A, "gated", i + 1)
            if v >= 2:
                wait(A, "down", v - 1)
            done(A.copy(guh[:, v % 2, h * 2 * UNIT:(h + 1) * 2 * UNIT], gu[:, i % 2, :]), "gu_hi")

        def dve_split(v, h):
            i = 2 * v + h
            wait(V, "gu_hi", i + 1)
            s = slice(h * 2 * UNIT, (h + 1) * 2 * UNIT)
            done(V.tensor_tensor(gul[:, v % 2, s], gu[:, i % 2, :], guh[:, v % 2, s], ALU.subtract), "gu_lo")

        def pe_down(v):
            wait(T, "gu_lo", 2 * v + 2)
            if v >= 2:
                wait(T, "y_out", v - 1)
            for t in range(TPU):
                o = psum[4 + v % 2][:, t * P:(t + 1) * P]
                for c in range(FC):
                    a, b = weights(v, 2, c)
                    s = slice(c * UNIT + t * P, c * UNIT + (t + 1) * P)
                    T.matmul(o, guh[:, v % 2, s], a, start=(c == 0), stop=False)
                    T.matmul(o, guh[:, v % 2, s], b, start=False, stop=False)
                    k = T.matmul(o, gul[:, v % 2, s], a, start=False, stop=(c == FC - 1))
            done(k, "down")

        def act_down(v):
            wait(A, "down", v + 1)
            src = psum[4 + v % 2][:, 0:UNIT]
            if not routed(v):
                if v == 0:
                    wait(A, "zeroed", 16 * zero_dmas)
                done(A.mul(ffn[:, v * TPU:(v + 1) * TPU, :].rearrange("p t d -> p (t d)"), src,
                           0.5 / 8 / SW / SW), "y_out")
            else:
                r = v - SHARED
                if r >= NYB:
                    wait(A, f"y_stored{r % NYB}", 16 * (r // NYB))
                done(A.mul(ybuf[:, r % NYB, :, :].rearrange("p t d -> p (t d)"), src, 1.0 / SW / SW), "y_out")

        def sp_down(v):
            r = v - SHARED
            if r >= 0:
                wait(nc.sync, "y_out", v + 1)
                done(nc.sync.dma_start(rows_out[r * UNIT:(r + 1) * UNIT, :].rearrange("(t p) d -> p t d", p=P),
                                       ybuf[:, r % NYB, :, :]), f"y_stored{r % NYB}", 16)

        def act_aconst():
            wait(A, "small_in", 80)
            done(A.activation(rate[:, :], dec[:, :], ACT.Exp), "rates")
            done(A.activation(rates[:, :], hdc[:, 0:HEADS], ACT.Exp), "rates")
            wait(A, "rates", 5)
            done(A.activation(wmat[:, :, :], wtmp[:, :, :], ACT.Exp, scale=-1.0), "decays")
            done(A.activation(wk[:, :].rearrange("p (h n) -> p h n", n=HD), rep(rates[:, :], HD), ACT.Exp,
                              scale=C("to_end")), "decays")
            done(A.activation(wb0[:, :], C("step"), ACT.Exp, scale=nrate[:, :]), "decays")
            done(A.activation(ws[:, :], rate[:, :], ACT.Exp, scale=-float(Q)), "decays")

        def dve_aconst():
            n = [0]

            def link(i):
                n[0] += 1
                done(i, "aconst")
                wait(V, "aconst", n[0])

            wait(V, "small_in", 80)
            wait(V, "rates", 2)
            done(V.tensor_scalar(rate[:, :], rate[:, :], 200.0, None, ALU.min), "rates")
            done(V.tensor_scalar(rates[:, :], rates[:, :], 200.0, None, ALU.min), "rates")
            wait(V, "rates", 4)
            link(V.tensor_scalar(nrate[:, :], rate[:, :], -1.0, None, ALU.mult))
            done(V.tensor_tensor(wtmp[:, :, :], rep(rates[:, :], Q), rep_mid(C("gap"), HEADS), ALU.mult), "rates")
            wait(V, "decays", 4)
            link(V.tensor_tensor(wmat[:, :, :], wmat[:, :, :], rep_mid(C("later"), HEADS), ALU.mult))
            link(V.tensor_tensor(wtmp[:, :, :], rep(hdc[:, HEADS:2 * HEADS], Q), rep_mid(C("same"), HEADS), ALU.mult))
            link(V.tensor_tensor(wmat[:, :, :], wmat[:, :, :], wtmp[:, :, :], ALU.add))
            link(V.tensor_scalar(wb[:, :], wb0[:, :], SY / SS / SW, None, ALU.mult))
            link(V.tensor_scalar(omx[:, :], mx[:, :], -1.0, 1.0, ALU.mult, ALU.add))
            for i in range(3):
                link(V.tensor_scalar(ws32[:, i, :], w32[:, i, :], omx[:, i:i + 1], SW, ALU.mult, ALU.mult))
                link(V.tensor_scalar(ws32[:, 3 + i, :], w32[:, i, :], mx[:, i:i + 1], SW, ALU.mult, ALU.mult))
            link(V.tensor_scalar(ws32[:, 6, :], w32[:, 3, :], SW, None, ALU.mult))
            link(V.tensor_copy(wph[:, :, :], ws32[:, :, :]))
            link(V.tensor_tensor(wpl[:, :, :], ws32[:, :, :], wph[:, :, :], ALU.subtract))
            link(V.tensor_scalar(brs[:, :], brk[:, :], SW, None, ALU.mult))
            wait(V, "bias_in", 32)
            link(V.tensor_scalar(bro[0:2, :], bro[0:2, :], SW, None, ALU.mult))
            link(V.tensor_copy(brh[0:2, :], bro[0:2, :]))
            link(V.tensor_tensor(brl[0:2, :], bro[0:2, :], brh[0:2, :], ALU.subtract))
            link(V.memset(brw[:, :], 0.0))
            link(V.tensor_scalar(bro[0:2, :], brh[0:2, :], C("ident")[0:2, 0:1], None, ALU.mult))
            link(V.scalar_tensor_tensor(brw[0:2, :], brl[0:2, :], C("ident")[0:2, 1:2], bro[0:2, :],
                                        ALU.mult, ALU.add))
            link(V.tensor_copy(f2[:, :], C("first2")))
            done(V.tensor_copy(f2y[:, :], C("first2y")), "aconst_ready")

        def dve_state0():
            wait(V, "down", NU)
            for t in (st, sh, sl):
                done(V.memset(t[:, :, :], 0.0), "ready")

        def sp_bias():
            for i in range(2):
                done(nc.sync.dma_start(bro[i:i + 1, :], bias_rows), "bias_in", 16)

        def where(u):
            return u // NG, u % NG

        def cols(t, g, shift):
            def of(tt):
                v = t[:, 4 * g * XS:4 * (g + 1) * XS].rearrange("p (b s) -> p b s", s=XS)
                return v[:, :, 2 + tt * P - shift:2 + (tt + 1) * P - shift]
            return of

        def bank_uses(u, k):
            return 5 * u + k

        def pe_proj(u, k):
            tt, g = where(u)
            n = prow(u, k)
            o = psum[n % 2]
            if n >= 2:
                wait(T, "proj_free", n - 1)
            if u == 0 and k == 0:
                wait(T, "ready", 3)
                wait(T, "zero_cols", 2 * nb)
                wait(T, "aconst_ready", 1)
            if k < 2:
                i = 0
                for shift in range(2):
                    mh, ml = cols(xh, g, shift)(tt), cols(xl, g, shift)(tt)
                    wsl = 3 * shift + k
                    for a, m in ((wph, mh), (wph, ml), (wpl, mh)):
                        j = T.matmul(o[:, :], a[:, wsl, :], m, start=(i == 0), stop=(i == 5))
                        i += 1
            else:
                for s in range(2):
                    b = 2 * (k - 2) + s
                    oo = o[:, s * 256:(s + 1) * 256]
                    T.matmul(oo, f2[:, :], brw[:, 0:256], start=True, stop=False)
                    i = 0
                    for shift in range(2):
                        ch, cl = cols(xh, g, shift)(tt)[:, b, :], cols(xl, g, shift)(tt)[:, b, :]
                        for a, m in ((ch, wph), (ch, wpl), (cl, wph)):
                            j = T.matmul(oo, a, m[:, 3 * shift + 1:3 * shift + 3, :].rearrange("p a d -> p (a d)"),
                                         start=False, stop=(i == 5))
                            i += 1
            done(j, "proj")

        proj_order = []

        def prow(u, k):
            return proj_order.index((u, k))

        def act_proj(u, k):
            n, s = prow(u, k), u % 2
            o = psum[n % 2]
            wait(A, "proj", n + 1)
            if u >= 2:
                wait(A, "av", 16 * (u - 1))
                wait(A, "inter", 4 * (u - 1))
                wait(A, "upd", 4 * (u - 1))
            if k < 2:
                done(A.activation((rh, kh)[k][:, s, :], o[:, :], ACT.Identity, bias=brs[:, k:k + 1]), "proj_hi")
            else:
                b = 2 * (k - 2)
                v3 = o[:, :].rearrange("p (s c) -> p s c", s=2)
                wait(A, "kdec", 2 * u + k - 1)
                done(A.copy(vh[:, s, b:b + 2, :], v3[:, :, P:2 * P]), "proj_hi")
                done(A.copy(kth[:, s, b:b + 2, :], kt[:, k % 2, :, :]), "kt_hi")

        def dve_proj1(u, k):
            n = prow(u, k)
            if k >= 2:
                wait(V, "proj", n + 1)
                if 2 * u + k - 2 >= 2:
                    wait(V, "kt_lo", 2 * u + k - 3)
                v3 = psum[n % 2][:, :].rearrange("p (s c) -> p s c", s=2)
                done(V.tensor_tensor(kt[:, k % 2, :, :], v3[:, :, 0:P], rep_mid(wk[:, :], 2), ALU.mult), "kdec")

        def dve_proj2(u, k):
            n, s = prow(u, k), u % 2
            o = psum[n % 2]
            m = 4 * u + k
            if k < 2:
                wait(V, "proj_hi", m + 1)
                hi, lo = ((rh, rl), (kh, kl))[k]
                done(V.scalar_tensor_tensor(lo[:, s, :], o[:, :], brs[:, k:k + 1], hi[:, s, :],
                                            ALU.add, ALU.subtract), "proj_free")
                if k == 0:
                    for q in range(HPG):
                        done(V.tensor_scalar(rmh[:, s, q, :], rh[:, s, :], C("slot")[:, q:q + 1], None, ALU.mult),
                             "rmask")
                    wait(V, "proj_free", n + 1)
                    for q in range(HPG):
                        done(V.tensor_scalar(rml[:, s, q, :], rl[:, s, :], C("slot")[:, q:q + 1], None, ALU.mult),
                             "rmask")
            else:
                b = 2 * (k - 2)
                wait(V, "kt_hi", 2 * u + k - 1)
                v3 = o[:, :].rearrange("p (s c) -> p s c", s=2)
                done(V.tensor_tensor(vl[:, s, b:b + 2, :], v3[:, :, P:2 * P], vh[:, s, b:b + 2, :], ALU.subtract),
                     "proj_free")
                done(V.tensor_tensor(ktl[:, s, b:b + 2, :], kt[:, k % 2, :, :], kth[:, s, b:b + 2, :], ALU.subtract),
                     "kt_lo")

        def pe_inter(u, c):
            tt, g = where(u)
            i = 4 * u + c
            if c == 0 and u >= 1:
                wait(T, "yint", u)
            before_updates = state_version(u, c)
            wait(T, "s_lo2", before_updates)
            wait(T, "proj_free", prow(u, 0) + 1)
            for b in range(4):
                o = psum[7][:, b * P + c * Q:b * P + (c + 1) * Q]
                S = slice(b * P, (b + 1) * P)
                R = slice(b * P + c * Q, b * P + (c + 1) * Q)
                T.matmul(o, sh[:, g, S], rh[:, u % 2, R], start=True, stop=False)
                T.matmul(o, sh[:, g, S], rl[:, u % 2, R], start=False, stop=False)
                k = T.matmul(o, sl[:, g, S], rh[:, u % 2, R], start=False, stop=True)
            done(k, "inter")

        def state_version(u, c):
            if c > 0:
                return 4 * u + c
            return 4 * (u - NG) + 4 if u >= NG else 0

        def pe_update(u, c):
            i = 4 * u + c
            wait(T, "kt_lo", 2 * u + 2)
            if i >= 1:
                wait(T, "um", i)
            R = slice(c * Q, (c + 1) * Q)
            for b in range(4):
                o = psum[6][:, b * P:(b + 1) * P]
                T.matmul(o, kth[R, u % 2, b, :], vh[R, u % 2, b, :], start=True, stop=False)
                T.matmul(o, kth[R, u % 2, b, :], vl[R, u % 2, b, :], start=False, stop=False)
                k = T.matmul(o, ktl[R, u % 2, b, :], vh[R, u % 2, b, :], start=False, stop=True)
            done(k, "upd")

        def dve_update(u, c):
            i = 4 * u + c
            wait(V, "upd", i + 1)
            if i >= 2:
                wait(V, "state", i - 1)
            done(V.tensor_tensor(um[:, i % 2, :].rearrange("p (b d) -> p b d", b=4),
                                 psum[6][:, :].rearrange("p (b d) -> p b d", b=4),
                                 rep_mid(C("head"), 4), ALU.mult), "um")

        def pool_update(u, c):
            i, g = 4 * u + c, where(u)[1]
            wait(V2, "um", i + 1)
            prev = state_version(u, c)
            wait(V2, "s_lo2", prev)
            done(V2.scalar_tensor_tensor(st[:, g, :], st[:, g, :], ws[:, 0:1], um[:, i % 2, :], ALU.mult, ALU.add),
                 "state")

        V2 = V

        def act_update(u, c):
            i, g = 4 * u + c, where(u)[1]
            wait(A, "state", i + 1)
            wait(A, "inter", i + 1)
            done(A.copy(sh[:, g, :], st[:, g, :]), "s_hi2")

        def pool_update2(u, c):
            i, g = 4 * u + c, where(u)[1]
            wait(G, "s_hi2", i + 1)
            done(G.tensor_tensor(sl[:, g, :], st[:, g, :], sh[:, g, :], ALU.subtract), "s_lo2")

        def pe_local_av(u, b):
            i, s = 4 * u + b, u % 2
            n, (vu, vb) = i - 1, divmod(i - 1, 4)
            vs = vu % 2
            for g in range(CH):
                if u < NA:
                    if g == 0:
                        wait(T, "rmask", 8 * (u + 1))
                        wait(T, "proj_free", prow(u, 1) + 1)
                        if i >= 2:
                            wait(T, "a_dec", i - 1)
                    R = slice(g * Q, (g + 1) * Q)
                    wait(T, "local", 4 * i + g)
                    for c in range(CH):
                        X = slice(b * P + c * Q, b * P + (c + 1) * Q)
                        o = psum[2 + i % 2][c * Q:(c + 1) * Q, g * P:(g + 1) * P]
                        T.matmul(o, kh[R, s, X], rmh[R, s, :, X], start=True, stop=False)
                        T.matmul(o, kh[R, s, X], rml[R, s, :, X], start=False, stop=False)
                        k = T.matmul(o, kl[R, s, X], rmh[R, s, :, X], start=False, stop=True)
                    done(k, "local")
                if n >= 0:
                    c = g
                    if c == 0:
                        wait(T, "a_lo", n + 1)
                        if n >= 2:
                            wait(T, "ysel", 4 * (n - 1))
                    R = slice(c * Q, (c + 1) * Q)
                    wait(T, "av", 4 * n + c)
                    for m in range(CH):
                        M, N = slice(m * Q, (m + 1) * Q), slice(m * P, (m + 1) * P)
                        o = psum[4 + n % 2][M, c * P:(c + 1) * P]
                        T.matmul(o, vh[R, vs, vb, M], ah[R, n % 2, N], start=True, stop=False)
                        T.matmul(o, vl[R, vs, vb, M], ah[R, n % 2, N], start=False, stop=False)
                        k = T.matmul(o, vh[R, vs, vb, M], al[R, n % 2, N], start=False, stop=True)
                    done(k, "av")

        def dve_local1(u, b):
            i = 4 * u + b
            wait(V, "local", 4 * (i + 1))
            if i >= 2:
                wait(V, "a_lo", i - 1)
            done(V.tensor_tensor(a32[:, i % 2, :], psum[2 + i % 2][:, :],
                                 wmat[:, :, :].rearrange("p h i -> p (h i)"), ALU.mult), "a_dec")

        def act_local(u, b):
            i = 4 * u + b
            wait(A, "a_dec", i + 1)
            if i >= 2:
                wait(A, "av", 4 * (i - 1))
            done(A.copy(ah[:, i % 2, :], a32[:, i % 2, :]), "a_hi")

        def dve_local2(u, b):
            i = 4 * u + b
            wait(V, "a_hi", i + 1)
            done(V.tensor_tensor(al[:, i % 2, :], a32[:, i % 2, :], ah[:, i % 2, :], ALU.subtract), "a_lo")

        def dve_av(u, b):
            i = 4 * u + b
            wait(V, "av", 4 * (i + 1))
            if u >= 2:
                wait(V, "y32", u - 1)
            y4 = psum[4 + i % 2][:, :].rearrange("p (c q i) -> p c q i", c=CH, q=HPG)
            acc = yacc[:, u % 2, b, :].rearrange("p (c i) -> p c i", c=CH)
            for q in range(HPG):
                m = C("slot_y")[:, q:q + 1]
                if q == 0:
                    done(V.tensor_scalar(acc, y4[:, :, q, :], m, None, ALU.mult), "ysel")
                else:
                    wait(V, "ysel", 4 * i + q)
                    done(V.scalar_tensor_tensor(acc, y4[:, :, q, :], m, acc, ALU.mult, ALU.add), "ysel")

        def dve_join1(u):
            s = u % 2
            wait(V, "inter", 4 * (u + 1))
            if u >= 2:
                wait(V, "y32", u - 1)
            done(V.tensor_tensor(yint[:, s, :].rearrange("p (a i) -> p a i", i=Q),
                                 psum[7][:, :].rearrange("p (a i) -> p a i", i=Q),
                                 rep_mid(wb[:, :], 16), ALU.mult), "yint")

        def dve_join2(u):
            s = u % 2
            wait(V, "yint", u + 1)
            wait(V, "ysel", 16 * (u + 1))
            if u >= 2:
                wait(V, "y_lo", u - 1)
            done(V.tensor_tensor(y32[:, s, :], yint[:, s, :], yacc[:, s, :, :].rearrange("p b d -> p (b d)"),
                                 ALU.add), "y32")

        def act_join(u):
            s = u % 2
            wait(A, "y32", u + 1)
            if u >= 2:
                wait(A, "proj", prow(u - 2, 4) + 1)
            done(A.copy(yh[:, s, :], y32[:, s, :]), "y_hi")

        def dve_join3(u):
            s = u % 2
            wait(V, "y_hi", u + 1)
            done(V.tensor_tensor(yl[:, s, :], y32[:, s, :], yh[:, s, :], ALU.subtract), "y_lo")

        def pe_out(u):
            s, n = u % 2, prow(u, 4)
            wait(T, "y_lo", u + 1)
            wait(T, "proj_free", n - 1)
            for b in range(4):
                o = psum[n % 2][:, b * P:(b + 1) * P]
                D = slice(b * P, (b + 1) * P)
                T.matmul(o, f2y[:, :], brw[:, 2 * P:3 * P], start=True, stop=False)
                T.matmul(o, yh[:, s, D], wph[:, 6, :], start=False, stop=False)
                T.matmul(o, yh[:, s, D], wpl[:, 6, :], start=False, stop=False)
                k = T.matmul(o, yl[:, s, D], wph[:, 6, :], start=False, stop=True)
            done(k, "proj")

        def tile(u, b):
            tt, g = where(u)
            return (4 * g + b) * TPS + tt

        def sp_fetch(u):
            tt, g = where(u)
            wait(nc.sync, "down", NU)
            if u >= 2:
                wait(nc.sync, "res", u - 1)
            done(nc.sync.dma_start(xin[:, u % 2, :, :], x_unit[g, tt]), f"x_again{u % 2}", 16)

        def pool_fetch(u):
            if u == 0:
                wait(G, "down", NU)
                for i in range(NYB):
                    wait(G, f"y_stored{i}", 16 * len(range(i, ROUTED, NYB)))
            if u >= 2:
                wait(G, "moe", 8 * (u - 1))
            for b in range(4):
                for k in range(2):
                    t = tile(u, b)
                    done(G.indirect_dma_start(picked[k][:, u % 2, b, :], None, rows_out,
                                              bass.IndirectOffsetOnAxis(pos[k][:, t:t + 1], 0)),
                         f"picked{u % 2}", 16)

        def dve_moe(u):
            s = u % 2
            wait(V, f"picked{s}", 16 * 8 * (u // 2 + 1))
            wait(V, "y_out", SHARED)
            wait(V, "gates", 2)
            if u >= 2:
                wait(V, "moe_silu", u - 1)
            for k in range(2):
                for b in range(4):
                    t = tile(u, b)
                    src = ffn[:, t, :] if k == 0 else mo[:, s, b, :]
                    done(V.scalar_tensor_tensor(mo[:, s, b, :], picked[k][:, s, b, :], gates[k][:, t:t + 1], src,
                                                ALU.mult, ALU.add), "moe")
                if k == 0:
                    wait(V, "moe", 8 * u + 4)

        def act_moe(u):
            s = u % 2
            wait(A, "moe", 8 * (u + 1))
            if u >= 2:
                wait(A, "res", u - 1)
            done(A.activation(gt[:, s, :], mo[:, s, :, :].rearrange("p b d -> p (b d)"), ACT.Silu), "moe_silu")

        def dve_end(u):
            s, n = u % 2, prow(u, 4)
            wait(V, "proj", n + 1)
            wait(V, "moe_silu", u + 1)
            if u >= 2:
                wait(V, f"stored{s}", 16 * (u // 2))
            done(V.scalar_tensor_tensor(res[:, s, :], psum[n % 2][:, :], 1.0 / SY / SW, gt[:, s, :],
                                        ALU.mult, ALU.mult), "proj_free")
            wait(V, "proj_free", n + 1)
            wait(V, f"x_again{s}", 16 * (u // 2 + 1))
            done(V.tensor_tensor(res[:, s, :], res[:, s, :], xin[:, s, :, :].rearrange("p b d -> p (b d)"),
                                 ALU.add), "res")

        def sp_end(u):
            tt, g = where(u)
            wait(nc.sync, "res", u + 1)
            done(nc.sync.dma_start(out_unit[g, tt], res[:, u % 2, :].rearrange("p (b d) -> p b d", b=4)),
                 f"stored{u % 2}", 16)

        stages = {
            "start": dict(sp=sp_start, dve=dve_prologue, pool=pool_prologue),
            "bias": dict(sp=sp_bias),
            "weights_in": dict(sp=sp_weights),
            "zero": dict(act=act_zero),
            "stats": dict(dve=dve_stats, act=act_std),
            "norm": dict(dve=dve_norm),
            "flip": dict(pe=pe_flip, act=act_flip),
            "flip2": dict(dve=dve_flip),
            "gate": dict(pe=pe_gate),
            "split_w": dict(act=act_split_w, dve=dve_split_w),
            "route": dict(dve=dve_route, act=act_route, pe=pe_route, pool=pool_scatter),
            "aconst": dict(act=act_aconst, dve=dve_aconst),
            "sorted_in": dict(sp=sp_sorted),
            "sorted": dict(pe=pe_sorted, act=act_sorted, dve=dve_sorted),
            "up": dict(pe=pe_up, act=act_up, dve=dve_up),
            "split": dict(act=act_split, dve=dve_split),
            "down": dict(pe=pe_down, act=act_down, sp=sp_down),
            "state0": dict(dve=dve_state0),
            "proj": dict(pe=pe_proj, act=act_proj, dve=dve_proj1),
            "proj2": dict(dve=dve_proj2),
            "inter": dict(pe=pe_inter),
            "update": dict(pe=pe_update, dve=dve_update),
            "state": dict(dve=pool_update, act=act_update, pool=pool_update2),
            "products": dict(pe=pe_local_av),
            "local": dict(dve=dve_local1, act=act_local),
            "local2": dict(dve=dve_local2),
            "av": dict(dve=dve_av),
            "join_state": dict(dve=dve_join1),
            "join": dict(dve=dve_join2, act=act_join),
            "join2": dict(dve=dve_join3),
            "out": dict(pe=pe_out),
            "fetch": dict(sp=sp_fetch, pool=pool_fetch),
            "moe": dict(dve=dve_moe, act=act_moe),
            "end": dict(dve=dve_end, sp=sp_end),
        }
        plan = [("start",), ("zero",), ("bias",)]
        plan += [("weights_in", 0), ("weights_in", 1)]
        for b in range(nb + 2):
            if b < nb:
                plan.append(("stats", b))
            if 1 <= b <= nb:
                plan += [("norm", b - 1), ("flip", b - 1)]
            if b >= 2:
                plan += [("flip2", b - 2), ("gate", b - 2)]
        plan.append(("route",))
        for e in range(EXPERTS + 1):
            plan.append(("split_w", e))
            if e + 2 <= EXPERTS:
                plan.append(("weights_in", e + 2))
        plan.append(("aconst",))
        for v in range(NU + 1):
            if v < NU:
                if routed(v):
                    for w in range(v + 2, v + 3) if v > SHARED else range(v, v + 3):
                        if w < NU:
                            plan.append(("sorted_in", w))
                    for w in range(v + 1, v + 2) if v > SHARED else range(v, v + 2):
                        if w < NU:
                            plan.append(("sorted", w))
                plan.append(("up", v, 0))
            if v > 0:
                plan.append(("split", v - 1, 1))
            if v < NU:
                plan.append(("up", v, 1))
            if v > 0:
                plan.append(("down", v - 1))
            if v < NU:
                plan.append(("split", v, 0))

        def proj(u, k):
            proj_order.append((u, k))
            return ("proj", u, k)

        plan += [("state0",), ("fetch", 0)]
        for k in range(4):
            plan += [proj(0, k), ("proj2", 0, k)]
        for u in range(NA + 1):
            for i in range(4):
                if u < NA:
                    plan += [("inter", u, i), ("update", u, i)]
                    if i == 1 and u + 1 < NA:
                        plan.append(("fetch", u + 1))
                    if u + 1 < NA:
                        plan.append(proj(u + 1, i))
                    plan.append(("state", u, i))
                if u < NA or i == 0:
                    plan.append(("products", u, i))
                if u < NA:
                    plan.append(("local", u, i))
                    if u + 1 < NA:
                        plan.append(("proj2", u + 1, i))
                last = (u, i - 1) if i else (u - 1, 3)
                if 0 <= last[0] < NA:
                    plan.append(("av", *last))
                if u < NA:
                    plan.append(("local2", u, i))
                    if i == 3:
                        plan.append(("join_state", u))
                if i == 0 and u > 0:
                    plan += [("join", u - 1), ("moe", u - 1)]
                if i == 1 and u > 0:
                    plan.append(("join2", u - 1))
                    proj_order.append((u - 1, 4))
                    plan += [("out", u - 1), ("end", u - 1)]

        def run(kind):
            for name, *args in plan:
                if kind in stages[name]:
                    stages[name][kind](*args)

        @block.sync
        def _(e):
            run("sp")
            for s in range(2):
                e.wait_ge(sem(f"stored{s}"), 16 * len(range(s, NA, 2)))

        @block.gpsimd
        def _(e):
            run("pool")

        @block.scalar
        def _(e):
            run("act")

        @block.vector
        def _(e):
            run("dve")

        @block.tensor
        def _(e):
            run("pe")


def kernel(**inputs):
    import concourse.bacc as bacc
    from concourse.bass_utils import run_bass_kernel_spmd

    a = {k[3:]: np.asarray(v) for k, v in inputs.items()}
    x = np.ascontiguousarray(a["attn_x"])
    nb = x.shape[0]
    arrays = {
        "x": x,
        "decay": np.repeat(a["attn_time_decay"], HD)[:, None],
        "per_head": np.broadcast_to(np.concatenate([a["attn_time_decay"], a["attn_time_faaaa"]]), (P, 2 * HEADS)),
        "maa": np.stack([a["attn_time_maa_r"], a["attn_time_maa_k"], a["attn_time_maa_v"]], 1),
        "wT": np.stack([a["attn_Wr"].T, a["attn_Wk"].T, a["attn_Wv"].T, a["attn_Wo"].T], 1),
        "bias": np.stack([a["attn_br"], a["attn_bk"]], 1),
        "bias_rows": np.concatenate([a["attn_bk"], a["attn_bv"], a["attn_bo"]])[None, :],
        "gateT": a["ffn_gate_W"].T,
        "w1e": a["ffn_w1_e"], "w3e": a["ffn_w3_e"], "w2e": a["ffn_w2_e"],
        "w1s": a["ffn_w1_s"], "w3s": a["ffn_w3_s"], "w2s": a["ffn_w2_s"],
        "const": constants(2 * nb * SEQ // UNIT + EXPERTS - 1),
    }
    arrays = {k: np.ascontiguousarray(v) for k, v in arrays.items()}
    nc = bacc.Bacc("TRN2", target_bir_lowering=False, num_devices=1)
    aps = {k: nc.dram_tensor(k, v.shape, mybir.dt.from_np(v.dtype), kind="ExternalInput").ap()
           for k, v in arrays.items()}
    out = nc.dram_tensor("out", x.shape, F32, kind="ExternalOutput").ap()
    build(nc, nb, *[aps[k] for k in arrays], out)
    return run_bass_kernel_spmd(nc, [arrays], core_ids=[0]).results[0]["out"]
```

```python
from contextlib import ExitStack

import numpy as np
import concourse.bass as bass
from concourse import mybir

F32, F16, I32 = mybir.dt.float32, mybir.dt.float16, mybir.dt.int32
ALU = mybir.AluOpType
ACT = mybir.ActivationFunctionType
AX = mybir.AxisListType.X

P = 128
HEADS, HD = 16, 8
Q = 32
CH = P // Q
HPG = Q // HD
SEQ = 512
TPS = SEQ // P
EXPERTS, WIDTH = 8, 512
FC = WIDTH // P
EW = 3 * WIDTH
UNIT = 256
XS = SEQ + 2

SW = 2.0 ** 8
SA = 2.0 ** 8
SS = 2.0 ** 4
SY = 2.0 ** 6

CONST = {}


def constants(routed):
    p = np.arange(P)
    j, i = p % Q, np.arange(Q)
    parts = {
        "ident": np.eye(P),
        "before": p[:, None] < p[None, :],
        "head": (p[:, None] // HD == p[None, :] // HD) * (SS / SW / SW),
        "first2": np.repeat(p[:, None] < 2, P, 1),
        "first2y": np.repeat(p[:, None] < 2, P, 1) * SY,
        "slot": (p[:, None] // HD) % HPG == np.arange(HPG)[None, :],
        "slot_y": ((p[:, None] // HD) % HPG == np.arange(HPG)[None, :]) * (SY / SA / SW),
        "gap": np.maximum(i[None, :] - j[:, None] - 1, 0),
        "later": (i[None, :] > j[:, None]) * (SA / SW / SW),
        "same": (i[None, :] == j[:, None]) * (SA / SW / SW),
        "step": np.repeat(i[None, :], P, 0),
        "to_end": -(Q - 1 - j[:, None]),
        "rank": np.repeat(EXPERTS - np.arange(EXPERTS)[None, :], P, 0),
        "units": np.repeat(UNIT * np.arange(routed)[None, :], P, 0),
        "ones": np.ones((P, 1)),
    }
    at, out = 0, []
    for name, a in parts.items():
        a = np.asarray(a, np.float32)
        CONST[name] = (at, a.shape[1])
        at += a.shape[1]
        out.append(a)
    return np.concatenate(out, 1)


def build(nc, nb, x, decay, per_head, maa, wT, bias, bias_rows, gateT, w1e, w3e, w2e, w1s, w3s, w2s, const, out):
    NTOK = nb * SEQ
    NT = NTOK // P
    SHARED = NTOK // UNIT
    ROUTED = 2 * NTOK // UNIT + EXPERTS - 1
    NU = SHARED + ROUTED
    NG = nb // 4
    NA = TPS * NG
    TPU = UNIT // P
    NTHR = NTOK // UNIT

    rows_in = nc.dram_tensor("sorted_rows", (ROUTED * UNIT, P), F32, kind="Internal").ap()
    rows_out = nc.dram_tensor("sorted_results", (ROUTED * UNIT, P), F32, kind="Internal").ap()

    ctx = ExitStack()
    with ctx:
        def sb(name, shape, dt=F32):
            return ctx.enter_context(nc.sbuf_tensor(name, shape, dt))

        def carve(*regions):
            left = [[r, 0] for r in regions]

            def take(shape, dt=F32):
                n = int(np.prod(shape[1:]))
                words = n if dt != F16 else n // 2
                for r in left:
                    if r[1] + words <= r[0].shape[1]:
                        v = r[0][:, r[1]:r[1] + words]
                        r[1] += words
                        break
                else:
                    raise ValueError("no room")
                if dt != F32:
                    v = v.bitcast(dt)
                names = "abc"[:len(shape) - 1]
                if len(names) > 1:
                    v = v.rearrange(f"p ({' '.join(names)}) -> p {' '.join(names)}", **dict(zip(names, shape[1:])))
                return v
            return take

        sems, waited = {}, {}

        def sem(name):
            if name not in sems:
                sems[name] = ctx.enter_context(nc.semaphore(name))
            return sems[name]

        def done(instruction, name, n=1):
            instruction.then_inc(sem(name), n)

        def wait(eng, name, n):
            key = (str(eng.engine), name)
            if n > waited.get(key, 0):
                waited[key] = n
                eng.wait_ge(sem(name), n)

        cst = sb("cst", [P, const.shape[1]])

        def C(name):
            at, n = CONST[name]
            return cst[:, at:at + n]

        rows = sb("rows", [P, NT, P])
        xh = sb("xh", [P, nb * XS], F16)
        xl = sb("xl", [P, nb * XS], F16)
        wwords = sb("wwords", [P, (EXPERTS + 1) * EW])
        wh = wwords[:, 0:wwords.shape[1] // 2].bitcast(F16)
        wl = wwords[:, wwords.shape[1] // 2:].bitcast(F16)
        stage = sb("stage", [P, 2, EW])
        ffn = sb("ffn", [P, NT, P])

        before = sb("before", [P, P], F16)
        ones16 = sb("ones16", [P, P], F16)
        stats = sb("stats", [P, NT, 6])
        mv = sb("mv", [P, NT, 2])
        vare = sb("vare", [P, NT])
        std = sb("std", [P, NT])
        rstd = sb("rstd", [P, NT])
        gate32 = sb("gate32", [P, EXPERTS])
        gateh = sb("gateh", [P, EXPERTS], F16)
        gatel = sb("gatel", [P, EXPERTS], F16)

        psum = [ctx.enter_context(nc.psum_tensor(f"bank{i}", [P, 512], F32)) for i in range(8)]

        NXB = 3
        srows = sb("srows", [P, NXB, TPU, P])
        sxh = sb("sxh", [P, NXB, UNIT], F16)
        sxl = sb("sxl", [P, NXB, UNIT], F16)
        hidden = sb("hidden", [P, 8 * 2 * UNIT])
        take = carve(hidden[:, :])
        sg = take([P, 2, 2 * UNIT])
        gu = take([P, 2, 2 * UNIT])
        guh = take([P, 2, FC * UNIT], F16)
        gul = take([P, 2, FC * UNIT], F16)
        NYB = 3
        ybuf = sb("ybuf", [P, NYB, TPU, P])

        take = carve(ffn[:, NT // 2:, :].rearrange("p a b -> p (a b)"))
        lg = take([P, NT, EXPERTS])
        ta = take([P, NT, EXPERTS])
        tb = take([P, NT, EXPERTS])
        oh = [take([P, NT, EXPERTS]) for k in range(2)]
        chosen = take([P, NT, EXPERTS], F16)
        top = [sb(f"top{k}", [P, NT]) for k in range(2)]
        tc_ = sb("tc_", [P, NT])
        zsum = sb("zsum", [P, NT])
        gates = [sb(f"gates{k}", [P, NT]) for k in range(2)]
        incl = take([P, EXPERTS, NT])
        posn = take([P, NT, EXPERTS])
        posf = sb("posf", [P, NT])
        pos = [sb(f"pos{k}", [P, NT], I32) for k in range(2)]
        early = carve(hidden[:, :])
        over = early([P, EXPERTS, NTHR])
        room = sb("room", [P, EXPERTS])
        ends = sb("ends", [P, EXPERTS])
        begins = sb("begins", [P, EXPERTS])
        eun = early([P, ROUTED, EXPERTS])
        eidf = sb("eidf", [P, ROUTED])
        eid = sb("eid", [P, ROUTED], I32)

        dec = sb("dec", [P, 1])
        hdc = sb("hdc", [P, 2 * HEADS])
        rate = sb("rate", [P, 1])
        nrate = sb("nrate", [P, 1])
        rates = sb("rates", [P, HEADS])
        wmat = sb("wmat", [P, HEADS, Q])
        wtmp = early([P, HEADS, Q])
        wk = sb("wk", [P, P])
        wb0 = early([P, Q])
        wb = sb("wb", [P, Q])
        ws = sb("ws", [P, 1])
        mx = sb("mx", [P, 3])
        omx = sb("omx", [P, 3])
        w32 = early([P, 4, P])
        ws32 = early([P, 7, P])
        wph = sb("wph", [P, 7, P], F16)
        wpl = sb("wpl", [P, 7, P], F16)
        brk = sb("brk", [P, 2])
        brs = sb("brs", [P, 2])
        brm = sb("brm", [P, HPG])
        bro = early([P, 3 * P])
        brh = early([P, 3 * P], F16)
        brl = early([P, 3 * P], F16)
        brw = sb("brw", [P, 3 * P], F16)
        f2 = sb("f2", [P, P], F16)
        f2y = sb("f2y", [P, P], F16)
        slot16 = sb("slot16", [P, HPG])

        take = carve(wwords[:, :], hidden[:, :], rows[:, :, :].rearrange("p a b -> p (a b)"),
                     stage[:, :, :].rearrange("p a b -> p (a b)"))
        r32 = take([P, 2, 512])
        rh = take([P, 2, 512], F16)
        rl = take([P, 2, 512], F16)
        rm = take([P, 2, HPG, 512])
        k32 = take([P, 2, 512])
        kt = take([P, 2, 2, P])
        kth = take([P, 2, 4, P], F16)
        ktl = take([P, 2, 4, P], F16)
        vh = take([P, 2, 4, P], F16)
        vl = take([P, 2, 4, P], F16)
        v32 = take([P, 2, 4, P])
        a32 = take([P, 2, 512])
        NUM = 3
        um = take([P, NUM, 512])
        st = take([P, NG, 2, 512])
        sh = take([P, 2, 512], F16)
        sl = take([P, 2, 512], F16)
        yacc = take([P, 2, 4, P])
        yint = take([P, 2, 512])
        y32 = take([P, 2, 512])
        yh = take([P, 2, 512], F16)
        yl = take([P, 2, 512], F16)
        picked = [take([P, 2, 4, P]) for k in range(2)]
        xin = take([P, 2, 4, P])
        mo = take([P, 2, 4, P])
        gt = take([P, 2, 512])
        res = take([P, 2, 512])

        x_rows = x.rearrange("b (t p) d -> b p t d", p=P)
        x_unit = x.rearrange("(g b) (t p) d -> g t p b d", b=4, p=P)
        out_unit = out.rearrange("(g b) (t p) d -> g t p b d", b=4, p=P)

        block = ctx.enter_context(nc.Block())
        pe, act, dve, pool, sp = {}, {}, {}, {}, {}
        V, A, T, G = nc.vector, nc.scalar, nc.tensor, nc.gpsimd

        def rep(ap, n):
            return ap.unsqueeze(2).to_broadcast([ap.shape[0], ap.shape[1], n])

        def rep_mid(ap, n):
            return ap.unsqueeze(1).to_broadcast([ap.shape[0], n, ap.shape[1]])

        def sp_start():
            for b in range(nb):
                done(nc.sync.dma_start(rows[:, b * TPS:(b + 1) * TPS, :], x_rows[b]), f"x_in{b}", 16)
                if b == 0:
                    done(nc.sync.dma_start(cst[:, :], const), "const_in", 16)
                    done(nc.sync.dma_start(gate32[:, :], gateT), "gate_in", 16)
                    for dst, src in ((dec, decay), (hdc, per_head), (mx, maa), (w32, wT), (brk, bias)):
                        done(nc.sync.dma_start(dst[:], src), "small_in", 16)

        def expert_of(k):
            return (k - 1) % (EXPERTS + 1)

        def sp_weights(k):
            s, e = k % 2, expert_of(k)
            if k >= 2:
                wait(nc.sync, "w_lo", k - 1)
            w1, w3, w2 = (w1s, w3s, w2s) if e == EXPERTS else (w1e[e], w3e[e], w2e[e])
            for i, w in enumerate((w1, w3, w2)):
                dst = stage[:, s, i * WIDTH:(i + 1) * WIDTH]
                if e == EXPERTS and i < 2:
                    w = w.rearrange("n d f -> d n f")
                    dst = dst.rearrange("p (n f) -> p n f", n=8)
                elif i == 2:
                    w = (w.rearrange("n f d -> (n f) d") if e == EXPERTS else w).rearrange("(c p) d -> p c d", p=P)
                    dst = dst.rearrange("p (c d) -> p c d", d=P)
                done(nc.sync.dma_start(dst, w), f"w_in{s}", 16)

        def sp_zero():
            wait(nc.sync, "zeros", 1)
            n = ROUTED * UNIT
            z = zero_rows
            flat = rows_in.rearrange("(p a) d -> p (a d)", p=P)
            width, at = flat.shape[1], 0
            while at < width:
                k = min(z.shape[1], width - at)
                done(nc.sync.dma_start(flat[:, at:at + k], z[:, 0:k]), "zeroed", 16)
                at += k

        zero_rows = ffn[:, 0:NT // 2, :].rearrange("p a b -> p (a b)")
        zero_dmas = -(-ROUTED * UNIT // (NT // 2 * P))

        def dve_prologue():
            done(V.memset(ffn[:, 0:NT // 2, :], 0.0), "zeros")
            wait(V, "const_in", 16)
            done(V.tensor_copy(before[:, :], C("before")), "tri")
            done(V.memset(ones16[:, :], 1.0), "tri")
            wait(V, "gate_in", 16)
            done(V.tensor_scalar(gate32[:, :], gate32[:, :], SW, None, ALU.mult), "gate_s")
            wait(V, "gate_s", 1)
            done(V.tensor_copy(gateh[:, :], gate32[:, :]), "gate_s")
            wait(V, "gate_s", 2)
            done(V.tensor_tensor(gatel[:, :], gate32[:, :], gateh[:, :], ALU.subtract), "gate_s")

        def pool_prologue():
            for t in (xh, xl):
                for b in range(nb):
                    done(G.memset(t[:, b * XS:b * XS + 2], 0.0), "zero_cols")

        def dve_stats(b):
            wait(V, f"x_in{b}", 16)
            for t in range(b * TPS, (b + 1) * TPS):
                done(V.bn_stats(stats[:, t, :], rows[:, t, :]), "bn")
            wait(V, "bn", (b + 1) * TPS)
            for t in range(b * TPS, (b + 1) * TPS):
                done(V.bn_aggr(mv[:, t, :], stats[:, t, :]), "mv")
            wait(V, "mv", (b + 1) * TPS)
            done(V.tensor_scalar(vare[:, b * TPS:(b + 1) * TPS], mv[:, b * TPS:(b + 1) * TPS, 1], 1e-5, None,
                                 ALU.add), "vare")

        def act_std(b):
            wait(A, "vare", b + 1)
            done(A.activation(std[:, b * TPS:(b + 1) * TPS], vare[:, b * TPS:(b + 1) * TPS], ACT.Sqrt), "std")

        def dve_norm(b):
            wait(V, "std", b + 1)
            done(V.reciprocal(rstd[:, b * TPS:(b + 1) * TPS], std[:, b * TPS:(b + 1) * TPS]), "rstd")
            wait(V, "rstd", b + 1)
            for t in range(b * TPS, (b + 1) * TPS):
                done(V.tensor_scalar(rows[:, t, :], rows[:, t, :], mv[:, t, 0:1], rstd[:, t:t + 1],
                                     ALU.subtract, ALU.mult), "normed")

        def pe_flip(b):
            wait(T, "const_in", 16)
            wait(T, "normed", (b + 1) * TPS)
            if b >= 4:
                wait(T, "x_lo", b - 3)
            for t in range(TPS):
                i = T.transpose(psum[b % 4][:, t * P:(t + 1) * P], rows[:, b * TPS + t, :], C("ident"))
            done(i, "flipped")

        def act_flip(b):
            wait(A, "flipped", b + 1)
            done(A.copy(xh[:, b * XS + 2:(b + 1) * XS], psum[b % 4][:, :]), "x_hi")

        def dve_flip(b):
            wait(V, "x_hi", b + 1)
            done(V.tensor_tensor(xl[:, b * XS + 2:(b + 1) * XS], psum[b % 4][:, :], xh[:, b * XS + 2:(b + 1) * XS],
                                 ALU.subtract), "x_lo")

        def pe_gate(b):
            wait(T, "gate_s", 3)
            wait(T, "x_lo", b + 1)
            for t in range(TPS):
                at = b * XS + 2 + t * P
                o = psum[7][:, (b * TPS + t) * EXPERTS:(b * TPS + t + 1) * EXPERTS]
                T.matmul(o, xh[:, at:at + P], gateh[:, :], start=True, stop=False)
                T.matmul(o, xh[:, at:at + P], gatel[:, :], start=False, stop=False)
                i = T.matmul(o, xl[:, at:at + P], gateh[:, :], start=False, stop=True)
            done(i, "logits")

        def act_split_w(k):
            s, e = k % 2, expert_of(k)
            wait(A, "w_scaled", k + 1)
            done(A.copy(wh[:, e * EW:(e + 1) * EW], stage[:, s, :]), "w_hi")

        def pool_split_w(k):
            s, e = k % 2, expert_of(k)
            wait(G, f"w_in{s}", 48 * (k // 2 + 1))
            done(G.tensor_scalar(stage[:, s, :], stage[:, s, :], SW, None, ALU.mult), "w_scaled")
            wait(G, "w_scaled", k + 1)
            wait(G, "w_hi", k + 1)
            done(G.tensor_tensor(wl[:, e * EW:(e + 1) * EW], stage[:, s, :], wh[:, e * EW:(e + 1) * EW],
                                 ALU.subtract), "w_lo")

        def dve_route():
            n = [0]

            def link(i):
                n[0] += 1
                done(i, "route")
                wait(V, "route", n[0])

            rank = C("rank").unsqueeze(1).to_broadcast([P, NT, EXPERTS])
            wait(V, "logits", nb)
            link(V.tensor_copy(lg[:, :, :], psum[7][:, 0:NT * EXPERTS].rearrange("p (t e) -> p t e", e=EXPERTS)))
            cur = lg
            for k in range(2):
                link(V.tensor_reduce(top[k][:, :], cur[:, :, :], AX, ALU.max))
                link(V.tensor_tensor(ta[:, :, :], cur[:, :, :], rep(top[k][:, :], EXPERTS), ALU.is_equal))
                link(V.tensor_tensor(ta[:, :, :], ta[:, :, :], rank, ALU.mult))
                link(V.tensor_reduce(tc_[:, :], ta[:, :, :], AX, ALU.max))
                link(V.tensor_tensor(oh[k][:, :, :], rep(tc_[:, :], EXPERTS), rank, ALU.is_equal))
                if k == 0:
                    link(V.scalar_tensor_tensor(tb[:, :, :], oh[0][:, :, :], -3e38, lg[:, :, :], ALU.mult, ALU.add))
                    cur = tb
            link(V.tensor_tensor(chosen[:, :, :], oh[0][:, :, :], oh[1][:, :, :], ALU.add))
            done(V.tensor_tensor(ta[:, :, :], lg[:, :, :], rep(top[0][:, :], EXPERTS), ALU.subtract), "shifted")
            done(V.tensor_tensor(tc_[:, :], top[1][:, :], top[0][:, :], ALU.subtract), "shifted")
            wait(V, "counts", 1)
            for e in range(EXPERTS):
                i = V.tensor_tensor_scan(
                    incl[:, e, :], C("ones").to_broadcast([P, NT]),
                    psum[1][:, 0:NT * EXPERTS].rearrange("p (t e) -> p e t", e=EXPERTS)[:, e, :],
                    0.0, ALU.mult, ALU.add)
                done(i, "scanned")
            wait(V, "scanned", EXPERTS)
            link(V.tensor_tensor(over[:, :, :], rep(incl[:, :, NT - 1], NTHR),
                                 rep_mid(C("units")[:, 0:NTHR], EXPERTS), ALU.is_gt))
            link(V.tensor_reduce(room[:, :], over[:, :, :], AX, ALU.add))
            link(V.tensor_scalar(room[:, :], room[:, :], float(UNIT), None, ALU.mult))
            link(V.tensor_tensor_scan(ends[:, :], C("ones").to_broadcast([P, EXPERTS]), room[:, :], 0.0,
                                      ALU.mult, ALU.add))
            link(V.tensor_tensor(begins[:, :], ends[:, :], room[:, :], ALU.subtract))
            link(V.tensor_tensor(eun[:, :, 1:EXPERTS], rep(C("units")[:, 0:ROUTED], EXPERTS - 1),
                                 rep_mid(begins[:, 1:EXPERTS], ROUTED), ALU.is_ge))
            link(V.tensor_reduce(eidf[:, :], eun[:, :, 1:EXPERTS], AX, ALU.add))
            done(V.tensor_copy(eid[:, :], eidf[:, :]), "unit_experts")
            tot = psum[1][:, 0:NT * EXPERTS].rearrange("p (t e) -> p t e", e=EXPERTS)
            cum = psum[0][:, 0:NT * EXPERTS].rearrange("p (t e) -> p t e", e=EXPERTS)
            link(V.tensor_tensor(posn[:, :, :], incl[:, :, :].rearrange("p e t -> p t e"), tot, ALU.subtract))
            link(V.tensor_tensor(posn[:, :, :], posn[:, :, :], cum, ALU.add))
            link(V.tensor_tensor(posn[:, :, :], posn[:, :, :], rep_mid(begins[:, :], NT), ALU.add))
            for k in range(2):
                link(V.tensor_tensor(tb[:, :, :], posn[:, :, :], oh[k][:, :, :], ALU.mult))
                link(V.tensor_reduce(posf[:, :], tb[:, :, :], AX, ALU.add))
                done(V.tensor_copy(pos[k][:, :], posf[:, :]), "places")
                wait(V, "places", k + 1)
            wait(V, "exps", 2)
            link(V.tensor_reduce(zsum[:, :], ta[:, :, :], AX, ALU.add))
            link(V.reciprocal(zsum[:, :], zsum[:, :]))
            done(V.tensor_scalar(gates[0][:, :], zsum[:, :], 0.5, None, ALU.mult), "gates")
            wait(V, "gates", 1)
            done(V.tensor_tensor(gates[1][:, :], tc_[:, :], gates[0][:, :], ALU.mult), "gates")

        def act_route():
            wait(A, "shifted", 2)
            done(A.activation(ta[:, :, :], ta[:, :, :], ACT.Exp, scale=1.0 / SW), "exps")
            done(A.activation(tc_[:, :], tc_[:, :], ACT.Exp, scale=1.0 / SW), "exps")

        ROUTE_CHOSEN = 1 + 5 * 2 + 1 + 1

        def pe_route():
            wait(T, "tri", 2)
            wait(T, "route", ROUTE_CHOSEN)
            m = chosen[:, :, :].rearrange("p t e -> p (t e)")
            T.matmul(psum[0][:, 0:NT * EXPERTS], before[:, :], m, start=True, stop=True)
            done(T.matmul(psum[1][:, 0:NT * EXPERTS], ones16[:, :], m, start=True, stop=True), "counts")

        def pool_scatter():
            wait(G, "places", 2)
            wait(G, "normed", NT)
            wait(G, "zeroed", 16 * zero_dmas)
            for t in range(NT):
                for k in range(2):
                    done(G.indirect_dma_start(rows_in, bass.IndirectOffsetOnAxis(pos[k][:, t:t + 1], 0),
                                              rows[:, t, :], None), "scattered", 16)

        def routed(v):
            return v >= SHARED

        def sp_sorted(v):
            r = v - SHARED
            wait(nc.sync, "scattered", 16 * 2 * NT)
            if r >= NXB:
                wait(nc.sync, "s_flipped", r - NXB + 1)
            done(nc.sync.dma_start(srows[:, r % NXB, :, :],
                                   rows_in[r * UNIT:(r + 1) * UNIT, :].rearrange("(t p) d -> p t d", p=P)),
                 f"s_in{r % NXB}", 16)

        def pe_sorted(v):
            r = v - SHARED
            wait(T, f"s_in{r % NXB}", 16 * (r // NXB + 1))
            if r == 0:
                wait(T, "route", ROUTE_CHOSEN)
            if r >= 2:
                wait(T, "s_lo", r - 1)
            for t in range(TPU):
                i = T.transpose(psum[6 + r % 2][:, t * P:(t + 1) * P], srows[:, r % NXB, t, :], C("ident"))
            done(i, "s_flipped")

        def act_sorted(v):
            r = v - SHARED
            wait(A, "s_flipped", r + 1)
            if r >= NXB:
                wait(A, "up", 2 * (v - NXB + 1))
            done(A.copy(sxh[:, r % NXB, :], psum[6 + r % 2][:, 0:UNIT]), "s_hi")

        def dve_sorted(v):
            r = v - SHARED
            wait(V, "s_hi", r + 1)
            done(V.tensor_tensor(sxl[:, r % NXB, :], psum[6 + r % 2][:, 0:UNIT], sxh[:, r % NXB, :],
                                 ALU.subtract), "s_lo")

        expert_at = {}

        def weights(v, part, c):
            at = part * WIDTH + c * P
            if not routed(v):
                at += EXPERTS * EW
                return wh[:, at:at + P], wl[:, at:at + P]
            d = bass.ds(expert_at[v] + at, P)
            return wh[:, d], wl[:, d]

        def pe_up(v, h):
            i = 2 * v + h
            if v == 0:
                wait(T, "w_lo", 1)
                wait(T, "places", 2)
            if routed(v):
                if h == 0:
                    wait(T, "w_lo", EXPERTS + 1)
                    wait(T, "unit_experts", 1)
                    expert_at[v] = T.value_load(eid[0:1, v - SHARED:v - SHARED + 1], min_val=0,
                                                max_val=EXPERTS - 1) * EW
                r = v - SHARED
                wait(T, "s_lo", r + 1)
                mh, ml = sxh[:, r % NXB, :], sxl[:, r % NXB, :]
            else:
                at = v * UNIT // SEQ * XS + 2 + v * UNIT % SEQ
                mh, ml = xh[:, at:at + UNIT], xl[:, at:at + UNIT]
            if i >= 2:
                wait(T, "gated", i - 1)
            for part in range(2):
                for c in range(2):
                    a, b = weights(v, part, 2 * h + c)
                    o = psum[2 * (i % 2) + part][:, c * UNIT:(c + 1) * UNIT]
                    T.matmul(o, a, mh, start=True, stop=False)
                    T.matmul(o, a, ml, start=False, stop=False)
                    k = T.matmul(o, b, mh, start=False, stop=True)
            done(k, "up")

        def act_up(v, h):
            i = 2 * v + h
            wait(A, "up", i + 1)
            if i == 0:
                wait(A, "aconst_ready", 1)
            if i >= 2:
                wait(A, "gated", i - 1)
            done(A.activation(sg[:, i % 2, :], psum[2 * (i % 2)][:, :], ACT.Silu, scale=1.0 / SW), "silu")

        def dve_up(v, h):
            i = 2 * v + h
            wait(V, "silu", i + 1)
            if i >= 2:
                wait(V, "gu_lo", i - 1)
            done(V.tensor_tensor(gu[:, i % 2, :], sg[:, i % 2, :], psum[2 * (i % 2) + 1][:, :], ALU.mult), "gated")

        def act_split(v, h):
            i = 2 * v + h
            wait(A, "gated", i + 1)
            if v >= 2:
                wait(A, "down", v - 1)
            done(A.copy(guh[:, v % 2, h * 2 * UNIT:(h + 1) * 2 * UNIT], gu[:, i % 2, :]), "gu_hi")

        def dve_split(v, h):
            i = 2 * v + h
            wait(V, "gu_hi", i + 1)
            s = slice(h * 2 * UNIT, (h + 1) * 2 * UNIT)
            done(V.tensor_tensor(gul[:, v % 2, s], gu[:, i % 2, :], guh[:, v % 2, s], ALU.subtract), "gu_lo")

        def pe_down(v):
            wait(T, "gu_lo", 2 * v + 2)
            if v >= 2:
                wait(T, "y_out", v - 1)
            for c in range(FC):
                a, b = weights(v, 2, c)
                for t in range(TPU):
                    o = psum[4 + v % 2][:, t * P:(t + 1) * P]
                    s = slice(c * UNIT + t * P, c * UNIT + (t + 1) * P)
                    T.matmul(o, guh[:, v % 2, s], a, start=(c == 0 and t == 0), stop=False)
                    T.matmul(o, guh[:, v % 2, s], b, start=False, stop=False)
                    k = T.matmul(o, gul[:, v % 2, s], a, start=False,
                                 stop=(c == FC - 1 and t == TPU - 1))
            done(k, "down")

        def act_down(v):
            wait(A, "down", v + 1)
            src = psum[4 + v % 2][:, 0:UNIT]
            if not routed(v):
                if v == 0:
                    wait(A, "zeroed", 16 * zero_dmas)
                done(A.mul(ffn[:, v * TPU:(v + 1) * TPU, :].rearrange("p t d -> p (t d)"), src,
                           0.5 / 8 / SW / SW), "y_out")
            else:
                r = v - SHARED
                if r >= NYB:
                    wait(A, f"y_stored{r % NYB}", 16 * (r // NYB))
                done(A.mul(ybuf[:, r % NYB, :, :].rearrange("p t d -> p (t d)"), src, 1.0 / SW / SW), "y_out")

        def sp_down(v):
            r = v - SHARED
            if r >= 0:
                wait(nc.sync, "y_out", v + 1)
                done(nc.sync.dma_start(rows_out[r * UNIT:(r + 1) * UNIT, :].rearrange("(t p) d -> p t d", p=P),
                                       ybuf[:, r % NYB, :, :]), f"y_stored{r % NYB}", 16)

        def act_aconst():
            wait(A, "small_in", 80)
            done(A.activation(rate[:, :], dec[:, :], ACT.Exp), "rates")
            done(A.activation(rates[:, :], hdc[:, 0:HEADS], ACT.Exp), "rates")
            wait(A, "rates", 5)
            done(A.activation(wmat[:, :, :], wtmp[:, :, :], ACT.Exp, scale=-1.0), "decays")
            done(A.activation(wk[:, :].rearrange("p (h n) -> p h n", n=HD), rep(rates[:, :], HD), ACT.Exp,
                              scale=C("to_end")), "decays")
            done(A.activation(wb0[:, :], C("step"), ACT.Exp, scale=nrate[:, :]), "decays")
            done(A.activation(ws[:, :], rate[:, :], ACT.Exp, scale=-float(Q)), "decays")

        def dve_aconst():
            n = [0]

            def link(i):
                n[0] += 1
                done(i, "aconst")
                wait(V, "aconst", n[0])

            wait(V, "small_in", 80)
            wait(V, "rates", 2)
            done(V.tensor_scalar(rate[:, :], rate[:, :], 200.0, None, ALU.min), "rates")
            done(V.tensor_scalar(rates[:, :], rates[:, :], 200.0, None, ALU.min), "rates")
            wait(V, "rates", 4)
            link(V.tensor_scalar(nrate[:, :], rate[:, :], -1.0, None, ALU.mult))
            done(V.tensor_tensor(wtmp[:, :, :], rep(rates[:, :], Q), rep_mid(C("gap"), HEADS), ALU.mult), "rates")
            wait(V, "decays", 4)
            link(V.tensor_tensor(wmat[:, :, :], wmat[:, :, :], rep_mid(C("later"), HEADS), ALU.mult))
            link(V.tensor_tensor(wtmp[:, :, :], rep(hdc[:, HEADS:2 * HEADS], Q), rep_mid(C("same"), HEADS), ALU.mult))
            link(V.tensor_tensor(wmat[:, :, :], wmat[:, :, :], wtmp[:, :, :], ALU.add))
            link(V.tensor_scalar(wb[:, :], wb0[:, :], SY / SS / SW, None, ALU.mult))
            link(V.tensor_scalar(omx[:, :], mx[:, :], -1.0, 1.0, ALU.mult, ALU.add))
            for i in range(3):
                link(V.tensor_scalar(ws32[:, i, :], w32[:, i, :], omx[:, i:i + 1], SW, ALU.mult, ALU.mult))
                link(V.tensor_scalar(ws32[:, 3 + i, :], w32[:, i, :], mx[:, i:i + 1], SW, ALU.mult, ALU.mult))
            link(V.tensor_scalar(ws32[:, 6, :], w32[:, 3, :], SW, None, ALU.mult))
            link(V.tensor_copy(wph[:, :, :], ws32[:, :, :]))
            link(V.tensor_tensor(wpl[:, :, :], ws32[:, :, :], wph[:, :, :], ALU.subtract))
            link(V.tensor_scalar(brs[:, :], brk[:, :], SW, None, ALU.mult))
            link(V.tensor_scalar(brm[:, :], C("slot"), brs[:, 0:1], None, ALU.mult))
            wait(V, "bias_in", 32)
            link(V.tensor_scalar(bro[0:2, :], bro[0:2, :], SW, None, ALU.mult))
            link(V.tensor_copy(brh[0:2, :], bro[0:2, :]))
            link(V.tensor_tensor(brl[0:2, :], bro[0:2, :], brh[0:2, :], ALU.subtract))
            link(V.memset(brw[:, :], 0.0))
            link(V.tensor_scalar(bro[0:2, :], brh[0:2, :], C("ident")[0:2, 0:1], None, ALU.mult))
            link(V.scalar_tensor_tensor(brw[0:2, :], brl[0:2, :], C("ident")[0:2, 1:2], bro[0:2, :],
                                        ALU.mult, ALU.add))
            link(V.tensor_copy(f2[:, :], C("first2")))
            done(V.tensor_copy(f2y[:, :], C("first2y")), "aconst_ready")

        def dve_state0():
            wait(V, "down", NU)
            done(V.memset(st[:, :, :, :], 0.0), "ready")

        def sp_bias():
            for i in range(2):
                done(nc.sync.dma_start(bro[i:i + 1, :], bias_rows), "bias_in", 16)

        def where(u):
            return u // NG, u % NG

        def cols(t, g, shift):
            def of(tt):
                v = t[:, 4 * g * XS:4 * (g + 1) * XS].rearrange("p (b s) -> p b s", s=XS)
                return v[:, :, 2 + tt * P - shift:2 + (tt + 1) * P - shift]
            return of

        PR, KV, PK, PO = 0, (1, 2), 3, 4
        proj_order = []

        def prow(u, k):
            return proj_order.index((u, k))

        def wait_left(eng, n):
            u, k = proj_order[n]
            if k in (PR, PK):
                wait(eng, "r32" if k == PR else "k32", u + 1)
            else:
                wait(eng, "proj_free", sum(kk not in (PR, PK) for _, kk in proj_order[:n + 1]))

        def pe_proj(u, k):
            tt, g = where(u)
            n = prow(u, k)
            o = psum[n % 2]
            if n >= 2:
                wait_left(T, n - 2)
            if u == 0 and k == 0:
                wait(T, "ready", 1)
                wait(T, "zero_cols", 2 * nb)
                wait(T, "aconst_ready", 1)
            if k not in KV:
                i = 0
                for shift in range(2):
                    mh, ml = cols(xh, g, shift)(tt), cols(xl, g, shift)(tt)
                    wsl = 3 * shift + (k == PK)
                    for a, m in ((wph, mh), (wph, ml), (wpl, mh)):
                        j = T.matmul(o[:, :], a[:, wsl, :], m, start=(i == 0), stop=(i == 5))
                        i += 1
            else:
                for s in range(2):
                    b = 2 * KV.index(k) + s
                    oo = o[:, s * 256:(s + 1) * 256]
                    T.matmul(oo, f2[:, :], brw[:, 0:256], start=True, stop=False)
                    i = 0
                    for shift in range(2):
                        ch, cl = cols(xh, g, shift)(tt)[:, b, :], cols(xl, g, shift)(tt)[:, b, :]
                        for a, m in ((ch, wph), (ch, wpl), (cl, wph)):
                            j = T.matmul(oo, a, m[:, 3 * shift + 1:3 * shift + 3, :].rearrange("p a d -> p (a d)"),
                                         start=False, stop=(i == 5))
                            i += 1
            done(j, "proj")

        def act_proj(u, k):
            n, s = prow(u, k), u % 2
            o = psum[n % 2]
            wait(A, "proj", n + 1)
            if u >= 2:
                wait(A, "local", 16 * (u - 1))
                wait(A, "inter", 4 * (u - 1))
                if k in KV:
                    wait(A, "av", 16 * (u - 1))
            if k in KV:
                i = KV.index(k)
                wait(A, "kdec", 2 * u + i + 1)
                v3 = o[:, :].rearrange("p (s c) -> p s c", s=2)
                done(A.copy(vh[:, s, 2 * i:2 * i + 2, :], v3[:, :, P:2 * P]), "v_hi")
                done(A.copy(v32[:, s, 2 * i:2 * i + 2, :], v3[:, :, P:2 * P]), "v32")
                done(A.copy(kth[:, s, 2 * i:2 * i + 2, :], kt[:, i, :, :]), "kt_hi")
            elif k == PR:
                if u >= 2:
                    wait(A, "r_lo", u - 1)
                done(A.activation(r32[:, s, :], o[:, :], ACT.Identity, bias=brs[:, 0:1]), "r32")
                wait(A, "r32", u + 1)
                done(A.copy(rh[:, s, :], r32[:, s, :]), "r_hi")
            else:
                done(A.activation(k32[:, s, :], o[:, :], ACT.Identity, bias=brs[:, 1:2]), "k32")

        def act_mask(u, q):
            s = u % 2
            done(A.mul(rm[:, s, q, :], r32[:, s, :], C("slot")[:, q:q + 1]), "rmask")

        def dve_proj1(u, k):
            n = prow(u, k)
            if k in KV:
                i = KV.index(k)
                wait(V, "proj", n + 1)
                if u >= 1:
                    wait(V, "kt_lo", 2 * u + i - 1)
                v3 = psum[n % 2][:, :].rearrange("p (s c) -> p s c", s=2)
                done(V.tensor_tensor(kt[:, i, :, :], v3[:, :, 0:P], rep_mid(wk[:, :], 2), ALU.mult), "kdec")

        def dve_proj2(u, k):
            n, s = prow(u, k), u % 2
            o = psum[n % 2]
            if k in KV:
                i = KV.index(k)
                b = slice(2 * i, 2 * i + 2)
                v3 = o[:, :].rearrange("p (s c) -> p s c", s=2)
                wait(V, "v_hi", 2 * u + i + 1)
                wait(V, "v32", 2 * u + i + 1)
                done(V.tensor_tensor(vl[:, s, b, :], v3[:, :, P:2 * P], vh[:, s, b, :], ALU.subtract),
                     "proj_free")
                wait(V, "kt_hi", 2 * u + i + 1)
                done(V.tensor_tensor(ktl[:, s, b, :], kt[:, i, :, :], kth[:, s, b, :], ALU.subtract),
                     "kt_lo")
            elif k == PR:
                wait(V, "r_hi", u + 1)
                done(V.tensor_tensor(rl[:, s, :], r32[:, s, :], rh[:, s, :], ALU.subtract), "r_lo")

        def of_step(j):
            return j // 4, j % 4, j // 4 % NG

        def last_step(j):
            u, c, _ = of_step(j)
            return j - 1 if c else 4 * (u - NG) + 3

        def version(j):
            u, c, _ = of_step(j)
            return (4 * where(u)[0] + c) % 2

        def pe_inter(j):
            u, c, g = of_step(j)
            if c == 0 and u >= 1:
                wait(T, "yint", u)
            wait(T, "state_lo", j + 1)
            wait(T, "r_lo", u + 1)
            for b in range(4):
                o = psum[7][:, b * P + c * Q:b * P + (c + 1) * Q]
                S = slice(b * P, (b + 1) * P)
                R = slice(b * P + c * Q, b * P + (c + 1) * Q)
                T.matmul(o, sh[:, j % 2, S], rh[:, u % 2, R], start=True, stop=False)
                T.matmul(o, sh[:, j % 2, S], rl[:, u % 2, R], start=False, stop=False)
                k = T.matmul(o, sl[:, j % 2, S], rh[:, u % 2, R], start=False, stop=True)
            done(k, "inter")

        def pe_update(j):
            u, c, g = of_step(j)
            wait(T, "kt_lo", 2 * u + 2)
            if j >= 1:
                wait(T, "um", j)
            R = slice(c * Q, (c + 1) * Q)
            for b in range(4):
                o = psum[6][:, b * P:(b + 1) * P]
                T.matmul(o, kth[R, u % 2, b, :], vh[R, u % 2, b, :], start=True, stop=False)
                T.matmul(o, kth[R, u % 2, b, :], vl[R, u % 2, b, :], start=False, stop=False)
                k = T.matmul(o, ktl[R, u % 2, b, :], vh[R, u % 2, b, :], start=False, stop=True)
            done(k, "upd")

        def dve_update(j):
            wait(V, "upd", j + 1)
            if j >= NUM:
                wait(V, "state", j - NUM + 1)
            done(V.tensor_tensor(um[:, j % NUM, :].rearrange("p (b d) -> p b d", b=4),
                                 psum[6][:, :].rearrange("p (b d) -> p b d", b=4),
                                 rep_mid(C("head"), 4), ALU.mult), "um")

        def dve_state(j):
            u, c, g = of_step(j)
            wait(V, "um", j + 1)
            if last_step(j) >= 0:
                wait(V, "state", last_step(j) + 1)
                wait(V, "state_lo", last_step(j) + 1)
            a = version(j)
            done(V.scalar_tensor_tensor(st[:, g, 1 - a, :], st[:, g, a, :], ws[:, 0:1], um[:, j % NUM, :],
                                        ALU.mult, ALU.add), "state")

        def act_state(j):
            u, c, g = of_step(j)
            if last_step(j) >= 0:
                wait(A, "state", last_step(j) + 1)
            else:
                wait(A, "ready", 1)
            if j >= 2:
                wait(A, "inter", j - 1)
            done(A.copy(sh[:, j % 2, :], st[:, g, version(j), :]), "state_hi")

        def pool_state(j):
            u, c, g = of_step(j)
            wait(G, "state_hi", j + 1)
            done(G.tensor_tensor(sl[:, j % 2, :], st[:, g, version(j), :], sh[:, j % 2, :], ALU.subtract),
                 "state_lo")

        def pe_local_av(u, b):
            i, s = 4 * u + b, u % 2
            n, (vu, vb) = i - 1, divmod(i - 1, 4)
            vs = vu % 2
            for g in range(CH):
                if u < NA:
                    if g == 0:
                        wait(T, "rmask", 4 * (u + 1))
                        wait(T, "k32", u + 1)
                        if i >= 2:
                            wait(T, "a_dec", i - 1)
                    R = slice(g * Q, (g + 1) * Q)
                    wait(T, "local", 4 * i + g)
                    for c in range(CH):
                        X = slice(b * P + c * Q, b * P + (c + 1) * Q)
                        k = T.matmul(psum[2 + i % 2][c * Q:(c + 1) * Q, g * P:(g + 1) * P],
                                     k32[R, s, X], rm[R, s, :, X], start=True, stop=True)
                    done(k, "local")
                if n >= 0:
                    c = g
                    if c == 0:
                        wait(T, "a_dec", n + 1)
                        if n >= 2:
                            wait(T, "ysel", 3 * (n - 1))
                    R = slice(c * Q, (c + 1) * Q)
                    wait(T, "av", 4 * n + c)
                    for m in range(CH):
                        M, N = slice(m * Q, (m + 1) * Q), slice(m * P, (m + 1) * P)
                        k = T.matmul(psum[4 + n % 2][M, c * P:(c + 1) * P],
                                     v32[R, vs, vb, M], a32[R, n % 2, N], start=True, stop=True)
                    done(k, "av")

        def dve_local(u, b):
            i = 4 * u + b
            wait(V, "local", 4 * (i + 1))
            if i >= 2:
                wait(V, "av", 4 * (i - 1))
            done(V.tensor_tensor(a32[:, i % 2, :], psum[2 + i % 2][:, :],
                                 wmat[:, :, :].rearrange("p h i -> p (h i)"), ALU.mult), "a_dec")

        def act_av(u, b):
            i = 4 * u + b
            wait(A, "av", 4 * (i + 1))
            if u >= 2:
                wait(A, "y32", u - 1)
            y4 = psum[4 + i % 2][:, :].rearrange("p (c q i) -> p c q i", c=CH, q=HPG)
            done(A.mul(yacc[:, u % 2, b, :].rearrange("p (c i) -> p c i", c=CH), y4[:, :, 0, :],
                       C("slot_y")[:, 0:1]), "ysel0")

        def dve_av(u, b):
            i = 4 * u + b
            wait(V, "ysel0", i + 1)
            y4 = psum[4 + i % 2][:, :].rearrange("p (c q i) -> p c q i", c=CH, q=HPG)
            acc = yacc[:, u % 2, b, :].rearrange("p (c i) -> p c i", c=CH)
            for q in range(1, HPG):
                m = C("slot_y")[:, q:q + 1]
                if q > 1:
                    wait(V, "ysel", 3 * i + q - 1)
                done(V.scalar_tensor_tensor(acc, y4[:, :, q, :], m, acc, ALU.mult, ALU.add), "ysel")

        def dve_join1(u):
            s = u % 2
            wait(V, "inter", 4 * (u + 1))
            done(V.tensor_tensor(yint[:, s, :].rearrange("p (a i) -> p a i", i=Q),
                                 psum[7][:, :].rearrange("p (a i) -> p a i", i=Q),
                                 rep_mid(wb[:, :], 16), ALU.mult), "yint")

        def dve_join2(u):
            s = u % 2
            wait(V, "yint", u + 1)
            wait(V, "ysel", 12 * (u + 1))
            if u >= 2:
                wait(V, "y_lo", u - 1)
            done(V.tensor_tensor(y32[:, s, :], yint[:, s, :], yacc[:, s, :, :].rearrange("p b d -> p (b d)"),
                                 ALU.add), "y32")

        def act_join(u):
            s = u % 2
            wait(A, "y32", u + 1)
            if u >= 2:
                wait(A, "proj", prow(u - 2, PO) + 1)
            done(A.copy(yh[:, s, :], y32[:, s, :]), "y_hi")

        def dve_join3(u):
            s = u % 2
            wait(V, "y_hi", u + 1)
            done(V.tensor_tensor(yl[:, s, :], y32[:, s, :], yh[:, s, :], ALU.subtract), "y_lo")

        def pe_out(u):
            s, n = u % 2, prow(u, PO)
            wait(T, "y_lo", u + 1)
            wait_left(T, n - 2)
            for b in range(4):
                o = psum[n % 2][:, b * P:(b + 1) * P]
                D = slice(b * P, (b + 1) * P)
                T.matmul(o, f2y[:, :], brw[:, 2 * P:3 * P], start=True, stop=False)
                T.matmul(o, yh[:, s, D], wph[:, 6, :], start=False, stop=False)
                T.matmul(o, yh[:, s, D], wpl[:, 6, :], start=False, stop=False)
                k = T.matmul(o, yl[:, s, D], wph[:, 6, :], start=False, stop=True)
            done(k, "proj")

        def tile(u, b):
            tt, g = where(u)
            return (4 * g + b) * TPS + tt

        def sp_fetch(u):
            tt, g = where(u)
            wait(nc.sync, "down", NU)
            if u >= 2:
                wait(nc.sync, "res", u - 1)
            done(nc.sync.dma_start(xin[:, u % 2, :, :], x_unit[g, tt]), f"x_again{u % 2}", 16)

        def pool_fetch(u, b):
            if u == 0 and b == 0:
                wait(G, "down", NU)
                for i in range(NYB):
                    wait(G, f"y_stored{i}", 16 * len(range(i, ROUTED, NYB)))
            if u >= 2:
                wait(G, "moe", 4 * (u - 1))
            t = tile(u, b)
            for k in range(2):
                done(G.indirect_dma_start(picked[k][:, u % 2, b, :], None, rows_out,
                                          bass.IndirectOffsetOnAxis(pos[k][:, t:t + 1], 0)),
                     f"picked{u % 2}", 16)

        def pool_moe(u, part):
            s = u % 2
            tt, g = where(u)

            def of_unit(a):
                v = a[:, 4 * g * TPS:4 * (g + 1) * TPS]
                if len(a.shape) == 2:
                    return v.rearrange("p (b t) -> p b t", t=TPS)[:, :, tt]
                return v.rearrange("p (b t) d -> p b t d", t=TPS)[:, :, tt, :]

            p0, p1, m = picked[0][:, s, :, :], picked[1][:, s, :, :], mo[:, s, :, :]
            if part == 0:
                wait(G, f"picked{s}", 16 * 8 * (u // 2 + 1))
                wait(G, "y_out", SHARED)
                wait(G, "gates", 2)
                i = G.tensor_tensor(p0, p0, rep(of_unit(gates[0]), P), ALU.mult)
            elif part == 1:
                i = G.tensor_tensor(p1, p1, rep(of_unit(gates[1]), P), ALU.mult)
            elif part == 2:
                if u >= 2:
                    wait(G, "moe_silu", u - 1)
                wait(G, "moe", 4 * u + 1)
                i = G.tensor_tensor(m, p0, of_unit(ffn), ALU.add)
            else:
                wait(G, "moe", 4 * u + 3)
                i = G.tensor_tensor(m, m, p1, ALU.add)
            done(i, "moe")

        def act_moe(u):
            s = u % 2
            wait(A, "moe", 4 * (u + 1))
            if u >= 2:
                wait(A, "res", u - 1)
            done(A.activation(gt[:, s, :], mo[:, s, :, :].rearrange("p b d -> p (b d)"), ACT.Silu), "moe_silu")

        def dve_end(u):
            s, n = u % 2, prow(u, PO)
            wait(V, "proj", n + 1)
            wait(V, "moe_silu", u + 1)
            if u >= 2:
                wait(V, f"stored{s}", 16 * (u // 2))
            done(V.scalar_tensor_tensor(res[:, s, :], psum[n % 2][:, :], 1.0 / SY / SW, gt[:, s, :],
                                        ALU.mult, ALU.mult), "proj_free")
            wait_left(V, n)
            wait(V, f"x_again{s}", 16 * (u // 2 + 1))
            done(V.tensor_tensor(res[:, s, :], res[:, s, :], xin[:, s, :, :].rearrange("p b d -> p (b d)"),
                                 ALU.add), "res")

        def sp_end(u):
            tt, g = where(u)
            wait(nc.sync, "res", u + 1)
            done(nc.sync.dma_start(out_unit[g, tt], res[:, u % 2, :].rearrange("p (b d) -> p b d", b=4)),
                 f"stored{u % 2}", 16)

        stages = {
            "start": dict(sp=sp_start, dve=dve_prologue, pool=pool_prologue),
            "bias": dict(sp=sp_bias),
            "weights_in": dict(sp=sp_weights),
            "zero": dict(sp=sp_zero),
            "stats": dict(dve=dve_stats, act=act_std),
            "norm": dict(dve=dve_norm),
            "flip": dict(pe=pe_flip, act=act_flip),
            "flip2": dict(dve=dve_flip),
            "gate": dict(pe=pe_gate),
            "split_w": dict(act=act_split_w, pool=pool_split_w),
            "route": dict(dve=dve_route, act=act_route, pe=pe_route, pool=pool_scatter),
            "aconst": dict(act=act_aconst, dve=dve_aconst),
            "sorted_in": dict(sp=sp_sorted),
            "sorted": dict(pe=pe_sorted, act=act_sorted, dve=dve_sorted),
            "up": dict(pe=pe_up, act=act_up, dve=dve_up),
            "split": dict(act=act_split, dve=dve_split),
            "down": dict(pe=pe_down, act=act_down, sp=sp_down),
            "state0": dict(dve=dve_state0),
            "proj": dict(pe=pe_proj, act=act_proj, dve=dve_proj1),
            "proj2": dict(dve=dve_proj2),
            "mask": dict(act=act_mask),
            "inter": dict(pe=pe_inter),
            "update": dict(pe=pe_update),
            "own_blocks": dict(dve=dve_update),
            "state": dict(dve=dve_state),
            "state_parts": dict(act=act_state, pool=pool_state),
            "products": dict(pe=pe_local_av),
            "local": dict(dve=dve_local),
            "av": dict(act=act_av, dve=dve_av),
            "join_state": dict(dve=dve_join1),
            "join": dict(dve=dve_join2, act=act_join),
            "join2": dict(dve=dve_join3),
            "out": dict(pe=pe_out),
            "x_again": dict(sp=sp_fetch),
            "fetch": dict(pool=pool_fetch),
            "moe": dict(pool=pool_moe),
            "gating": dict(act=act_moe),
            "end": dict(dve=dve_end, sp=sp_end),
        }
        plan = [("start",), ("bias",), ("weights_in", 0), ("weights_in", 1), ("zero",)]
        split = 0
        for b in range(nb + 2):
            if b < nb:
                plan.append(("stats", b))
            if 1 <= b <= nb:
                plan += [("norm", b - 1), ("flip", b - 1)]
            if b >= 2:
                plan += [("flip2", b - 2), ("gate", b - 2)]
            if (b >= nb // 2 or b >= 6) and split <= EXPERTS:
                plan.append(("split_w", split))
                if split + 2 <= EXPERTS:
                    plan.append(("weights_in", split + 2))
                split += 1
        for k in range(split, EXPERTS + 1):
            plan.append(("split_w", k))
            if k + 2 <= EXPERTS:
                plan.append(("weights_in", k + 2))
        plan.append(("route",))
        plan.append(("aconst",))
        for v in range(NU + 1):
            if v < NU:
                if routed(v):
                    for w in range(v + 2, v + 3) if v > SHARED else range(v, v + 3):
                        if w < NU:
                            plan.append(("sorted_in", w))
                    for w in range(v + 1, v + 2) if v > SHARED else range(v, v + 2):
                        if w < NU:
                            plan.append(("sorted", w))
                for h in range(2):
                    plan += [("up", v, h), ("split", v, h)]
            if v > 0:
                plan.append(("down", v - 1))

        def proj(u, k):
            proj_order.append((u, k))
            return ("proj", u, k)

        plan += [("state0",), ("x_again", 0)]
        for k in range(4):
            plan += [proj(0, k), ("proj2", 0, k), ("mask", 0, k)]
        plan += [("state_parts", 0), ("update", 0), ("own_blocks", 0), ("update", 1), ("own_blocks", 1)]
        plan += [("fetch", 0, b) for b in range(4)]
        NJ = 4 * NA
        for u in range(NA + 1):
            for i in range(4 if u < NA else 3):
                j = 4 * u + i
                now, more = u < NA, u + 1 < NA
                if now:
                    plan += [("inter", j), ("state", j)]
                    if i == 3:
                        plan.append(("join_state", u))
                    if j + 1 < NJ:
                        plan.append(("state_parts", j + 1))
                    plan.append(("moe", u, i))
                if more:
                    plan += [proj(u + 1, i), ("fetch", u + 1, i)]
                    if i == 0:
                        plan.append(("x_again", u + 1))
                if i == 2 and u > 0:
                    proj_order.append((u - 1, PO))
                    plan.append(("out", u - 1))
                if now or i == 0:
                    plan.append(("products", u, i))
                if now and j + 2 < NJ:
                    plan.append(("update", j + 2))
                if more:
                    plan += [("proj2", u + 1, i), ("mask", u + 1, i)]
                if now:
                    plan.append(("local", u, i))
                if i == 2 and u > 0:
                    plan.append(("end", u - 1))
                if now and j + 2 < NJ:
                    plan.append(("own_blocks", j + 2))
                last = (u, i - 1) if i else (u - 1, 3)
                if 0 <= last[0] < NA:
                    plan.append(("av", *last))
                if i == 0 and u > 0:
                    plan += [("join", u - 1), ("gating", u - 1)]
                if i == 1 and u > 0:
                    plan.append(("join2", u - 1))

        def run(kind):
            for name, *args in plan:
                if kind in stages[name]:
                    stages[name][kind](*args)

        @block.sync
        def _(e):
            run("sp")
            for s in range(2):
                e.wait_ge(sem(f"stored{s}"), 16 * len(range(s, NA, 2)))

        @block.gpsimd
        def _(e):
            run("pool")

        @block.scalar
        def _(e):
            run("act")

        @block.vector
        def _(e):
            run("dve")

        @block.tensor
        def _(e):
            run("pe")


def kernel(**inputs):
    import concourse.bacc as bacc
    from concourse.bass_utils import run_bass_kernel_spmd

    a = {k[3:]: np.asarray(v) for k, v in inputs.items()}
    x = np.ascontiguousarray(a["attn_x"])
    nb = x.shape[0]
    arrays = {
        "x": x,
        "decay": np.repeat(a["attn_time_decay"], HD)[:, None],
        "per_head": np.broadcast_to(np.concatenate([a["attn_time_decay"], a["attn_time_faaaa"]]), (P, 2 * HEADS)),
        "maa": np.stack([a["attn_time_maa_r"], a["attn_time_maa_k"], a["attn_time_maa_v"]], 1),
        "wT": np.stack([a["attn_Wr"].T, a["attn_Wk"].T, a["attn_Wv"].T, a["attn_Wo"].T], 1),
        "bias": np.stack([a["attn_br"], a["attn_bk"]], 1),
        "bias_rows": np.concatenate([a["attn_bk"], a["attn_bv"], a["attn_bo"]])[None, :],
        "gateT": a["ffn_gate_W"].T,
        "w1e": a["ffn_w1_e"], "w3e": a["ffn_w3_e"], "w2e": a["ffn_w2_e"],
        "w1s": a["ffn_w1_s"], "w3s": a["ffn_w3_s"], "w2s": a["ffn_w2_s"],
        "const": constants(2 * nb * SEQ // UNIT + EXPERTS - 1),
    }
    arrays = {k: np.ascontiguousarray(v) for k, v in arrays.items()}
    nc = bacc.Bacc("TRN2", target_bir_lowering=False, num_devices=1)
    aps = {k: nc.dram_tensor(k, v.shape, mybir.dt.from_np(v.dtype), kind="ExternalInput").ap()
           for k, v in arrays.items()}
    out = nc.dram_tensor("out", x.shape, F32, kind="ExternalOutput").ap()
    build(nc, nb, *[aps[k] for k in arrays], out)
    return run_bass_kernel_spmd(nc, [arrays], core_ids=[0]).results[0]["out"]
```

```python
from contextlib import ExitStack

import numpy as np
import concourse.bass as bass
from concourse import mybir

F32, F16, I32 = mybir.dt.float32, mybir.dt.float16, mybir.dt.int32
ALU = mybir.AluOpType
ACT = mybir.ActivationFunctionType
AX = mybir.AxisListType.X

P = 128
HEADS, HD = 16, 8
Q = 32
CH = P // Q
HPG = Q // HD
SEQ = 512
TPS = SEQ // P
EXPERTS, WIDTH = 8, 512
FC = WIDTH // P
EW = 3 * WIDTH
UNIT = 256
XS = SEQ + 2

SW = 2.0 ** 8
SS = 2.0 ** 4
SY = 2.0 ** 6

CONST = {}


def constants(routed):
    p = np.arange(P)
    j, i = p % Q, np.arange(Q)
    parts = {
        "ident": np.eye(P),
        "not_before": -(p[:, None] >= p[None, :]).astype(np.float32),
        "head": (p[:, None] // HD == p[None, :] // HD) * (SS / SW / SW),
        "first2": np.repeat(p[:, None] < 2, P, 1),
        "first2y": np.repeat(p[:, None] < 2, P, 1) * SY,
        "slot": (p[:, None] // HD) % HPG == np.arange(HPG)[None, :],
        "slot_y": ((p[:, None] // HD) % HPG == np.arange(HPG)[None, :]) * (SY / SW),
        "gap": np.maximum(i[None, :] - j[:, None] - 1, 0),
        "later": (i[None, :] > j[:, None]) / (SW * SW),
        "same": (i[None, :] == j[:, None]) / (SW * SW),
        "step": np.repeat(i[None, :], P, 0),
        "to_end": -(Q - 1 - j[:, None]),
        "rank": np.repeat(EXPERTS - np.arange(EXPERTS)[None, :], P, 0),
        "units": np.repeat(UNIT * np.arange(routed)[None, :], P, 0),
        "ones": np.ones((P, 1)),
    }
    at, out = 0, []
    for name, a in parts.items():
        a = np.asarray(a, np.float32)
        CONST[name] = (at, a.shape[1])
        at += a.shape[1]
        out.append(a)
    return np.concatenate(out, 1)


def build(nc, nb, x, decay, per_head, maa, wT, bias, bias_rows, gateT, w1e, w3e, w2e, w1s, w3s, w2s, const, out):
    NTOK = nb * SEQ
    NT = NTOK // P
    SHARED = NTOK // UNIT
    ROUTED = 2 * NTOK // UNIT + EXPERTS - 1
    NU = SHARED + ROUTED
    NG = nb // 4
    NA = TPS * NG
    TPU = UNIT // P
    NTHR = NTOK // UNIT

    rows_in = nc.dram_tensor("sorted_rows", (ROUTED * UNIT, P), F32, kind="Internal").ap()
    rows_out = nc.dram_tensor("sorted_results", (ROUTED * UNIT, P), F32, kind="Internal").ap()

    ctx = ExitStack()
    with ctx:
        def sb(name, shape, dt=F32):
            return ctx.enter_context(nc.sbuf_tensor(name, shape, dt))

        def carve(*regions):
            left = [[r, 0] for r in regions]

            def take(shape, dt=F32):
                n = int(np.prod(shape[1:]))
                words = n if dt != F16 else n // 2
                for r in left:
                    if r[1] + words <= r[0].shape[1]:
                        v = r[0][:, r[1]:r[1] + words]
                        r[1] += words
                        break
                else:
                    raise ValueError("no room")
                if dt != F32:
                    v = v.bitcast(dt)
                names = "abc"[:len(shape) - 1]
                if len(names) > 1:
                    v = v.rearrange(f"p ({' '.join(names)}) -> p {' '.join(names)}", **dict(zip(names, shape[1:])))
                return v
            return take

        sems, waited = {}, {}

        def sem(name):
            if name not in sems:
                sems[name] = ctx.enter_context(nc.semaphore(name))
            return sems[name]

        def done(instruction, name, n=1):
            instruction.then_inc(sem(name), n)

        def wait(eng, name, n):
            key = (str(eng.engine), name)
            if n > waited.get(key, 0):
                waited[key] = n
                eng.wait_ge(sem(name), n)

        cst = sb("cst", [P, const.shape[1]])

        def C(name):
            at, n = CONST[name]
            return cst[:, at:at + n]

        rows = sb("rows", [P, NT, P])
        xh = sb("xh", [P, nb * XS], F16)
        xl = sb("xl", [P, nb * XS], F16)
        wwords = sb("wwords", [P, (EXPERTS + 1) * EW])
        FREE_EXPERTS = 3
        wh = wwords[:, 0:wwords.shape[1] // 2].bitcast(F16)
        wl = wwords[:, wwords.shape[1] // 2:].bitcast(F16)
        stage = sb("stage", [P, 2, EW])
        ffn = sb("ffn", [P, NT, P])

        not_before = sb("not_before", [P, P], F16)
        ones16 = sb("ones16", [P, P], F16)
        stats = sb("stats", [P, NT, 6])
        mv = sb("mv", [P, NT, 2])
        vare = sb("vare", [P, NT])
        std = sb("std", [P, NT])
        rstd = sb("rstd", [P, NT])
        shift = sb("shift", [P, NT])
        gate32 = sb("gate32", [P, EXPERTS])
        gateh = sb("gateh", [P, EXPERTS], F16)
        gatel = sb("gatel", [P, EXPERTS], F16)

        psum = [ctx.enter_context(nc.psum_tensor(f"bank{i}", [P, 512], F32)) for i in range(8)]

        NXB = 3
        srows = sb("srows", [P, NXB, TPU, P])
        sxh = sb("sxh", [P, NXB, UNIT], F16)
        sxl = sb("sxl", [P, NXB, UNIT], F16)
        hidden = sb("hidden", [P, 8 * 2 * UNIT])
        take = carve(hidden[:, :])
        sg = take([P, 2, 2 * UNIT])
        gu = take([P, 2, 2 * UNIT])
        guh = take([P, 2, FC * UNIT], F16)
        gul = take([P, 2, FC * UNIT], F16)
        NYB = 3
        ybuf = sb("ybuf", [P, NYB, TPU, P])

        take = carve(ffn[:, NT // 2:, :].rearrange("p a b -> p (a b)"))
        lg = take([P, NT, EXPERTS])
        ta = take([P, NT, EXPERTS])
        tb = take([P, NT, EXPERTS])
        oh = [take([P, NT, EXPERTS]) for k in range(2)]
        chosen = take([P, NT, EXPERTS], F16)
        top = [sb(f"top{k}", [P, NT]) for k in range(2)]
        pick = sb("pick", [P, NT])
        zsum = sb("zsum", [P, NT])
        gates = [sb(f"gates{k}", [P, NT]) for k in range(2)]
        incl = take([P, EXPERTS, NT])
        posn = take([P, NT, EXPERTS])
        posf = sb("posf", [P, NT])
        pos = [sb(f"pos{k}", [P, NT], I32) for k in range(2)]
        early = carve(wwords[:, FREE_EXPERTS * EW // 2:EXPERTS * EW // 2])
        over = early([P, EXPERTS, NTHR])
        room = sb("room", [P, EXPERTS])
        ends = sb("ends", [P, EXPERTS])
        begins = sb("begins", [P, EXPERTS])
        eun = early([P, ROUTED, EXPERTS])
        eidf = sb("eidf", [P, ROUTED])
        eid = sb("eid", [P, ROUTED], I32)

        dec = sb("dec", [P, 1])
        hdc = sb("hdc", [P, 2 * HEADS])
        rate = sb("rate", [P, 1])
        nrate = sb("nrate", [P, 1])
        rates = sb("rates", [P, HEADS])
        wmat = sb("wmat", [P, HEADS, Q])
        wtmp = early([P, HEADS, Q])
        wk = sb("wk", [P, P])
        wb0 = early([P, Q])
        wb = sb("wb", [P, Q])
        ws = sb("ws", [P, 1])
        mx = sb("mx", [P, 3])
        omx = sb("omx", [P, 3])
        w32 = early([P, 4, P])
        ws32 = early([P, 7, P])
        wph = sb("wph", [P, 7, P], F16)
        wpl = sb("wpl", [P, 7, P], F16)
        brk = sb("brk", [P, 2])
        brs = sb("brs", [P, 2])
        bro = early([P, 3 * P])
        brh = early([P, 3 * P], F16)
        brl = early([P, 3 * P], F16)
        brw = sb("brw", [P, 3 * P], F16)
        f2 = sb("f2", [P, P], F16)
        f2y = sb("f2y", [P, P], F16)

        take = carve(stage[:, :, :].rearrange("p a b -> p (a b)"), wwords[:, :], hidden[:, :],
                     rows[:, :, :].rearrange("p a b -> p (a b)"))
        first_state = take([P, NG, 512])
        r32 = take([P, 2, 512])
        rh = take([P, 2, 512], F16)
        rl = take([P, 2, 512], F16)
        rm = take([P, 2, HPG, 512])
        k32 = take([P, 2, 512])
        kt = take([P, 2, 2, P])
        kth = take([P, 2, 4, P], F16)
        ktl = take([P, 2, 4, P], F16)
        vh = take([P, 2, 4, P], F16)
        vl = take([P, 2, 4, P], F16)
        v32 = take([P, 2, 4, P])
        a32 = take([P, 2, 512])
        NUM = 3
        um = take([P, NUM, 512])
        st = [first_state, take([P, NG, 512])]
        sh = take([P, 2, 512], F16)
        sl = take([P, 2, 512], F16)
        yacc = take([P, 2, 4, P])
        yint = take([P, 2, 512])
        y32 = take([P, 2, 512])
        yh = take([P, 2, 512], F16)
        yl = take([P, 2, 512], F16)
        picked = [take([P, 2, 4, P]) for k in range(2)]
        xin = take([P, 2, 4, P])
        mo = take([P, 2, 4, P])
        gt = take([P, 2, 512])
        res = take([P, 2, 512])

        x_rows = x.rearrange("b (t p) d -> b p t d", p=P)
        x_unit = x.rearrange("(g b) (t p) d -> g t p b d", b=4, p=P)
        out_unit = out.rearrange("(g b) (t p) d -> g t p b d", b=4, p=P)

        block = ctx.enter_context(nc.Block())
        pe, act, dve, pool, sp = {}, {}, {}, {}, {}
        V, A, T, G = nc.vector, nc.scalar, nc.tensor, nc.gpsimd

        def rep(ap, n):
            return ap.unsqueeze(2).to_broadcast([ap.shape[0], ap.shape[1], n])

        def rep_mid(ap, n):
            return ap.unsqueeze(1).to_broadcast([ap.shape[0], n, ap.shape[1]])

        def sp_start():
            for b in range(nb):
                done(nc.sync.dma_start(rows[:, b * TPS:(b + 1) * TPS, :], x_rows[b]), f"x_in{b}", 16)
                if b == 0:
                    done(nc.sync.dma_start(cst[:, :], const), "const_in", 16)
                    done(nc.sync.dma_start(gate32[:, :], gateT), "gate_in", 16)
                    for dst, src in ((dec, decay), (hdc, per_head), (mx, maa), (w32, wT), (brk, bias)):
                        done(nc.sync.dma_start(dst[:], src), "small_in", 16)

        def expert_of(k):
            return (k - 1) % (EXPERTS + 1)

        def sp_weights(k):
            s, e = k % 2, expert_of(k)
            if k >= 2:
                wait(nc.sync, "w_lo", 3 * (k - 1))
            w1, w3, w2 = (w1s, w3s, w2s) if e == EXPERTS else (w1e[e], w3e[e], w2e[e])
            for i, w in enumerate((w1, w3, w2)):
                dst = stage[:, s, i * WIDTH:(i + 1) * WIDTH]
                if e == EXPERTS and i < 2:
                    w = w.rearrange("n d f -> d n f")
                    dst = dst.rearrange("p (n f) -> p n f", n=8)
                elif i == 2:
                    w = (w.rearrange("n f d -> (n f) d") if e == EXPERTS else w).rearrange("(c p) d -> p c d", p=P)
                    dst = dst.rearrange("p (c d) -> p c d", d=P)
                done(nc.sync.dma_start(dst, w), f"w_in{s}", 16)

        def sp_zero():
            wait(nc.sync, "zeros", 1)
            n = ROUTED * UNIT
            z = zero_rows
            flat = rows_in.rearrange("(p a) d -> p (a d)", p=P)
            width, at = flat.shape[1], 0
            while at < width:
                k = min(z.shape[1], width - at)
                done(nc.sync.dma_start(flat[:, at:at + k], z[:, 0:k]), "zeroed", 16)
                at += k

        zero_rows = ffn[:, 0:NT // 2, :].rearrange("p a b -> p (a b)")
        zero_dmas = -(-ROUTED * UNIT // (NT // 2 * P))

        def dve_prologue():
            wait(V, "const_in", 16)
            done(V.tensor_copy(not_before[:, :], C("not_before")), "tri")
            done(V.memset(ones16[:, :], 1.0), "tri")
            wait(V, "gate_in", 16)
            done(V.tensor_scalar(gate32[:, :], gate32[:, :], SW, None, ALU.mult), "gate_s")
            wait(V, "gate_s", 1)
            done(V.tensor_copy(gateh[:, :], gate32[:, :]), "gate_s")
            wait(V, "gate_s", 2)
            done(V.tensor_tensor(gatel[:, :], gate32[:, :], gateh[:, :], ALU.subtract), "gate_s")

        def pool_prologue():
            done(G.memset(ffn[:, 0:NT // 2, :], 0.0), "zeros")
            for t in (xh, xl):
                for b in range(nb):
                    done(G.memset(t[:, b * XS:b * XS + 2], 0.0), "zero_cols")

        def dve_stats(b):
            wait(V, f"x_in{b}", 16)
            for t in range(b * TPS, (b + 1) * TPS):
                done(V.bn_stats(stats[:, t, :], rows[:, t, :]), "bn")
            wait(V, "bn", (b + 1) * TPS)
            for t in range(b * TPS, (b + 1) * TPS):
                done(V.bn_aggr(mv[:, t, :], stats[:, t, :]), "mv")
            wait(V, "mv", (b + 1) * TPS)
            done(V.tensor_scalar(vare[:, b * TPS:(b + 1) * TPS], mv[:, b * TPS:(b + 1) * TPS, 1], 1e-5, None,
                                 ALU.add), "vare")

        def act_std(b):
            wait(A, "vare", b + 1)
            done(A.activation(std[:, b * TPS:(b + 1) * TPS], vare[:, b * TPS:(b + 1) * TPS], ACT.Sqrt), "std")

        def dve_norm(b):
            T4 = slice(b * TPS, (b + 1) * TPS)
            wait(V, "std", b + 1)
            done(V.reciprocal(rstd[:, T4], std[:, T4]), "rstd")
            wait(V, "rstd", b + 1)
            done(V.scalar_tensor_tensor(shift[:, T4], mv[:, T4, 0], -1.0, rstd[:, T4], ALU.mult, ALU.mult),
                 "shift")

        def act_norm(b):
            wait(A, "shift", b + 1)
            for t in range(b * TPS, b * TPS + TPS // 2):
                done(A.activation(rows[:, t, :], rows[:, t, :], ACT.Identity, bias=shift[:, t:t + 1],
                                  scale=rstd[:, t:t + 1]), "normed_a")

        def pool_norm(b):
            wait(G, "shift", b + 1)
            for t in range(b * TPS + TPS // 2, (b + 1) * TPS):
                done(G.tensor_scalar(rows[:, t, :], rows[:, t, :], rstd[:, t:t + 1], shift[:, t:t + 1],
                                     ALU.mult, ALU.add), "normed_g")

        def pe_flip(b):
            wait(T, "const_in", 16)
            wait(T, "normed_a", (b + 1) * TPS // 2)
            wait(T, "normed_g", (b + 1) * TPS // 2)
            if b >= 4:
                wait(T, "x_lo", b - 3)
            for t in range(TPS):
                i = T.transpose(psum[b % 4][:, t * P:(t + 1) * P], rows[:, b * TPS + t, :], C("ident"))
            done(i, "flipped")

        def act_flip(b):
            wait(A, "flipped", b + 1)
            done(A.copy(xh[:, b * XS + 2:(b + 1) * XS], psum[b % 4][:, :]), "x_hi")

        def dve_flip(b):
            wait(V, "x_hi", b + 1)
            done(V.tensor_tensor(xl[:, b * XS + 2:(b + 1) * XS], psum[b % 4][:, :], xh[:, b * XS + 2:(b + 1) * XS],
                                 ALU.subtract), "x_lo")

        def pe_gate(b):
            wait(T, "gate_s", 3)
            wait(T, "x_lo", b + 1)
            for t in range(TPS):
                at = b * XS + 2 + t * P
                o = psum[7][:, (b * TPS + t) * EXPERTS:(b * TPS + t + 1) * EXPERTS]
                T.matmul(o, xh[:, at:at + P], gateh[:, :], start=True, stop=False)
                T.matmul(o, xh[:, at:at + P], gatel[:, :], start=False, stop=False)
                i = T.matmul(o, xl[:, at:at + P], gateh[:, :], start=False, stop=True)
            done(i, "logits")

        def act_split_w(k, part):
            s, e = k % 2, expert_of(k)
            wait(A, f"w_in{s}", 48 * (k // 2 + 1))
            if FREE_EXPERTS <= e < EXPERTS:
                wait(A, "aconst_ready", 1)
                wait(A, "unit_experts", 1)
            at = part * WIDTH
            done(A.mul(wh[:, e * EW + at:e * EW + at + WIDTH], stage[:, s, at:at + WIDTH], SW), "w_hi")

        def dve_split_w(k, part):
            s, e = k % 2, expert_of(k)
            wait(V, "w_hi", 3 * k + part + 1)
            wait(V, f"w_in{s}", 48 * (k // 2 + 1))
            at = part * WIDTH
            done(V.scalar_tensor_tensor(wl[:, e * EW + at:e * EW + at + WIDTH], stage[:, s, at:at + WIDTH], SW,
                                        wh[:, e * EW + at:e * EW + at + WIDTH], ALU.mult, ALU.subtract), "w_lo")

        def route_steps():
            n = [0]

            def link(i):
                n[0] += 1
                done(i, "route")
                wait(V, "route", n[0])

            rank = C("rank").unsqueeze(1).to_broadcast([P, NT, EXPERTS])
            wait(V, "logits", nb)
            link(V.tensor_copy(lg[:, :, :], psum[7][:, 0:NT * EXPERTS].rearrange("p (t e) -> p t e", e=EXPERTS)))
            yield
            cur = lg
            for k in range(2):
                link(V.tensor_reduce(top[k][:, :], cur[:, :, :], AX, ALU.max))
                yield
                link(V.tensor_tensor(ta[:, :, :], cur[:, :, :], rep(top[k][:, :], EXPERTS), ALU.is_equal))
                yield
                link(V.tensor_tensor(ta[:, :, :], ta[:, :, :], rank, ALU.mult))
                yield
                link(V.tensor_reduce(pick[:, :], ta[:, :, :], AX, ALU.max))
                yield
                link(V.tensor_tensor(oh[k][:, :, :], rep(pick[:, :], EXPERTS), rank, ALU.is_equal))
                yield
                if k == 0:
                    link(V.scalar_tensor_tensor(tb[:, :, :], oh[0][:, :, :], -3e38, lg[:, :, :], ALU.mult, ALU.add))
                    yield
                    cur = tb
            link(V.tensor_tensor(chosen[:, :, :], oh[0][:, :, :], oh[1][:, :, :], ALU.add))
            yield
            done(V.tensor_tensor(ta[:, :, :], lg[:, :, :], rep(top[0][:, :], EXPERTS), ALU.subtract), "shifted")
            done(V.tensor_tensor(pick[:, :], top[1][:, :], top[0][:, :], ALU.subtract), "shifted")
            yield
            wait(V, "counts", 1)
            for e in range(EXPERTS):
                i = V.tensor_tensor_scan(
                    incl[:, e, :], C("ones").to_broadcast([P, NT]),
                    psum[7][:, 0:NT * EXPERTS].rearrange("p (t e) -> p e t", e=EXPERTS)[:, e, :],
                    0.0, ALU.mult, ALU.add)
                done(i, "scanned")
            wait(V, "scanned", EXPERTS)
            link(V.tensor_tensor(over[:, :, :], rep(incl[:, :, NT - 1], NTHR),
                                 rep_mid(C("units")[:, 0:NTHR], EXPERTS), ALU.is_gt))
            yield
            link(V.tensor_reduce(room[:, :], over[:, :, :], AX, ALU.add))
            yield
            link(V.tensor_scalar(room[:, :], room[:, :], float(UNIT), None, ALU.mult))
            yield
            link(V.tensor_tensor_scan(ends[:, :], C("ones").to_broadcast([P, EXPERTS]), room[:, :], 0.0,
                                      ALU.mult, ALU.add))
            yield
            link(V.tensor_tensor(begins[:, :], ends[:, :], room[:, :], ALU.subtract))
            yield
            link(V.tensor_tensor(posn[:, :, :], psum[6][:, 0:NT * EXPERTS].rearrange("p (t e) -> p t e", e=EXPERTS),
                                 incl[:, :, :].rearrange("p e t -> p t e"), ALU.add))
            yield
            link(V.tensor_tensor(posn[:, :, :], posn[:, :, :], rep_mid(begins[:, :], NT), ALU.add))
            yield
            for k in range(2):
                link(V.tensor_tensor(tb[:, :, :], posn[:, :, :], oh[k][:, :, :], ALU.mult))
                yield
                link(V.tensor_reduce(posf[:, :], tb[:, :, :], AX, ALU.add))
                yield
                done(V.tensor_copy(pos[k][:, :], posf[:, :]), "places")
                wait(V, "places", k + 1)
            link(V.tensor_tensor(eun[:, :, 1:EXPERTS], rep(C("units")[:, 0:ROUTED], EXPERTS - 1),
                                 rep_mid(begins[:, 1:EXPERTS], ROUTED), ALU.is_ge))
            yield
            link(V.tensor_reduce(eidf[:, :], eun[:, :, 1:EXPERTS], AX, ALU.add))
            yield
            done(V.tensor_copy(eid[:, :], eidf[:, :]), "unit_experts")
            wait(V, "exps", 2)
            link(V.tensor_reduce(zsum[:, :], ta[:, :, :], AX, ALU.add))
            yield
            link(V.reciprocal(zsum[:, :], zsum[:, :]))
            yield
            done(V.tensor_scalar(gates[0][:, :], zsum[:, :], 0.5, None, ALU.mult), "gates")
            wait(V, "gates", 1)
            done(V.tensor_tensor(gates[1][:, :], pick[:, :], gates[0][:, :], ALU.mult), "gates")

        running = {}

        def dve_steps(steps, n):
            if steps not in running:
                running[steps] = steps()
            for i in range(n):
                next(running[steps], None)

        def act_route():
            wait(A, "shifted", 2)
            done(A.activation(ta[:, :, :], ta[:, :, :], ACT.Exp, scale=1.0 / SW), "exps")
            done(A.activation(pick[:, :], pick[:, :], ACT.Exp, scale=1.0 / SW), "exps")

        ROUTE_CHOSEN = 1 + 5 * 2 + 1 + 1
        ROUTE_PLACES = 5 + 2 + 4

        def pe_route():
            wait(T, "tri", 2)
            wait(T, "route", ROUTE_CHOSEN)
            m = chosen[:, :, :].rearrange("p t e -> p (t e)")
            T.matmul(psum[6][:, 0:NT * EXPERTS], not_before[:, :], m, start=True, stop=True)
            done(T.matmul(psum[7][:, 0:NT * EXPERTS], ones16[:, :], m, start=True, stop=True), "counts")

        def pool_scatter():
            wait(G, "normed_a", NT // 2)
            wait(G, "normed_g", NT // 2)
            wait(G, "zeroed", 16 * zero_dmas)
            for k in range(2):
                wait(G, "places", k + 1)
                for t in range(NT):
                    done(G.indirect_dma_start(rows_in, bass.IndirectOffsetOnAxis(pos[k][:, t:t + 1], 0),
                                              rows[:, t, :], None), "scattered", 16)

        def routed(v):
            return v >= SHARED

        def sp_sorted(v):
            r = v - SHARED
            wait(nc.sync, "scattered", 16 * 2 * NT)
            if r >= NXB:
                wait(nc.sync, "s_flipped", r - NXB + 1)
            done(nc.sync.dma_start(srows[:, r % NXB, :, :],
                                   rows_in[r * UNIT:(r + 1) * UNIT, :].rearrange("(t p) d -> p t d", p=P)),
                 f"s_in{r % NXB}", 16)

        def pe_sorted(v):
            r = v - SHARED
            wait(T, f"s_in{r % NXB}", 16 * (r // NXB + 1))
            if r == 0:
                wait(T, "places", 2)
            if r >= 2:
                wait(T, "s_lo", r - 1)
            for t in range(TPU):
                i = T.transpose(psum[6 + r % 2][:, t * P:(t + 1) * P], srows[:, r % NXB, t, :], C("ident"))
            done(i, "s_flipped")

        def act_sorted(v):
            r = v - SHARED
            wait(A, "s_flipped", r + 1)
            if r >= NXB:
                wait(A, "up", 2 * (v - NXB + 1))
            done(A.copy(sxh[:, r % NXB, :], psum[6 + r % 2][:, 0:UNIT]), "s_hi")

        def dve_sorted(v):
            r = v - SHARED
            wait(V, "s_hi", r + 1)
            done(V.tensor_tensor(sxl[:, r % NXB, :], psum[6 + r % 2][:, 0:UNIT], sxh[:, r % NXB, :],
                                 ALU.subtract), "s_lo")

        expert_at = {}

        def weights(v, part, c):
            at = part * WIDTH + c * P
            if not routed(v):
                at += EXPERTS * EW
                return wh[:, at:at + P], wl[:, at:at + P]
            d = bass.ds(expert_at[v] + at, P)
            return wh[:, d], wl[:, d]

        def pe_expert(v):
            wait(T, "unit_experts", 1)
            r = v - SHARED
            expert_at[v] = T.value_load(eid[0:1, r:r + 1], min_val=0, max_val=EXPERTS - 1) * EW

        def pe_up(v, h):
            i = 2 * v + h
            if v == 0:
                wait(T, "w_lo", 3)
                wait(T, "x_lo", nb)
            if routed(v):
                if h == 0:
                    wait(T, "w_lo", 3 * (EXPERTS + 1))
                r = v - SHARED
                wait(T, "s_lo", r + 1)
                mh, ml = sxh[:, r % NXB, :], sxl[:, r % NXB, :]
            else:
                at = v * UNIT // SEQ * XS + 2 + v * UNIT % SEQ
                mh, ml = xh[:, at:at + UNIT], xl[:, at:at + UNIT]
            if i >= 2:
                wait(T, "gated", i - 1)
            for part in range(2):
                for c in range(2):
                    if (h, part, c) == (1, 1, 0) and v + 1 < NU and routed(v + 1):
                        pe_expert(v + 1)
                    a, b = weights(v, part, 2 * h + c)
                    o = psum[2 * (i % 2) + part][:, c * UNIT:(c + 1) * UNIT]
                    T.matmul(o, a, mh, start=True, stop=False)
                    T.matmul(o, a, ml, start=False, stop=False)
                    k = T.matmul(o, b, mh, start=False, stop=True)
            done(k, "up")

        def act_up(v, h):
            i = 2 * v + h
            wait(A, "up", i + 1)
            if i >= 2:
                wait(A, "gated", i - 1)
            done(A.activation(sg[:, i % 2, :], psum[2 * (i % 2)][:, :], ACT.Silu, scale=1.0 / SW), "silu")

        def dve_up(v, h):
            i = 2 * v + h
            wait(V, "silu", i + 1)
            if i >= 2:
                wait(V, "gu_lo", i - 1)
            done(V.tensor_tensor(gu[:, i % 2, :], sg[:, i % 2, :], psum[2 * (i % 2) + 1][:, :], ALU.mult), "gated")

        def act_split(v, h):
            i = 2 * v + h
            wait(A, "gated", i + 1)
            if v >= 2:
                wait(A, "down", v - 1)
            done(A.copy(guh[:, v % 2, h * 2 * UNIT:(h + 1) * 2 * UNIT], gu[:, i % 2, :]), "gu_hi")

        def dve_split(v, h):
            i = 2 * v + h
            wait(V, "gu_hi", i + 1)
            s = slice(h * 2 * UNIT, (h + 1) * 2 * UNIT)
            done(V.tensor_tensor(gul[:, v % 2, s], gu[:, i % 2, :], guh[:, v % 2, s], ALU.subtract), "gu_lo")

        def pe_down(v):
            wait(T, "gu_lo", 2 * v + 2)
            if v >= 2:
                wait(T, "y_out", v - 1)
            for c in range(FC):
                a, b = weights(v, 2, c)
                for t in range(TPU):
                    o = psum[4 + v % 2][:, t * P:(t + 1) * P]
                    s = slice(c * UNIT + t * P, c * UNIT + (t + 1) * P)
                    T.matmul(o, guh[:, v % 2, s], a, start=(c == 0 and t == 0), stop=False)
                    T.matmul(o, guh[:, v % 2, s], b, start=False, stop=False)
                    k = T.matmul(o, gul[:, v % 2, s], a, start=False,
                                 stop=(c == FC - 1 and t == TPU - 1))
            done(k, "down")

        def act_down(v):
            wait(A, "down", v + 1)
            src = psum[4 + v % 2][:, 0:UNIT]
            if not routed(v):
                if v == 0:
                    wait(A, "zeroed", 16 * zero_dmas)
                done(A.mul(ffn[:, v * TPU:(v + 1) * TPU, :].rearrange("p t d -> p (t d)"), src,
                           0.5 / 8 / SW / SW), "y_out")
            else:
                r = v - SHARED
                if r >= NYB:
                    wait(A, f"y_stored{r % NYB}", 16 * (r // NYB))
                done(A.mul(ybuf[:, r % NYB, :, :].rearrange("p t d -> p (t d)"), src, 1.0 / SW / SW), "y_out")

        def sp_down(v):
            r = v - SHARED
            if r >= 0:
                wait(nc.sync, "y_out", v + 1)
                done(nc.sync.dma_start(rows_out[r * UNIT:(r + 1) * UNIT, :].rearrange("(t p) d -> p t d", p=P),
                                       ybuf[:, r % NYB, :, :]), f"y_stored{r % NYB}", 16)

        def act_rates():
            wait(A, "small_in", 80)
            done(A.activation(rate[:, :], dec[:, :], ACT.Exp), "rates")
            done(A.activation(rates[:, :], hdc[:, 0:HEADS], ACT.Exp), "rates")

        def act_decays():
            wait(A, "rates", 5)
            done(A.activation(wmat[:, :, :], wtmp[:, :, :], ACT.Exp, scale=-1.0), "decays")
            done(A.activation(wk[:, :].rearrange("p (h n) -> p h n", n=HD), rep(rates[:, :], HD), ACT.Exp,
                              scale=C("to_end")), "decays")
            done(A.activation(wb0[:, :], C("step"), ACT.Exp, scale=nrate[:, :]), "decays")
            done(A.activation(ws[:, :], rate[:, :], ACT.Exp, scale=-float(Q)), "decays")

        def aconst_steps():
            n = [0]

            def link(i):
                n[0] += 1
                done(i, "aconst")
                wait(V, "aconst", n[0])

            wait(V, "small_in", 80)
            wait(V, "rates", 2)
            done(V.tensor_scalar(rate[:, :], rate[:, :], 200.0, None, ALU.min), "rates")
            done(V.tensor_scalar(rates[:, :], rates[:, :], 200.0, None, ALU.min), "rates")
            wait(V, "rates", 4)
            link(V.tensor_scalar(nrate[:, :], rate[:, :], -1.0, None, ALU.mult))
            done(V.tensor_tensor(wtmp[:, :, :], rep(rates[:, :], Q), rep_mid(C("gap"), HEADS), ALU.mult), "rates")
            yield
            wait(V, "decays", 4)
            link(V.tensor_tensor(wmat[:, :, :], wmat[:, :, :], rep_mid(C("later"), HEADS), ALU.mult))
            yield
            link(V.tensor_tensor(wtmp[:, :, :], rep(hdc[:, HEADS:2 * HEADS], Q), rep_mid(C("same"), HEADS), ALU.mult))
            yield
            link(V.tensor_tensor(wmat[:, :, :], wmat[:, :, :], wtmp[:, :, :], ALU.add))
            yield
            link(V.tensor_scalar(wb[:, :], wb0[:, :], SY / SS / SW, None, ALU.mult))
            yield
            link(V.tensor_scalar(omx[:, :], mx[:, :], -1.0, 1.0, ALU.mult, ALU.add))
            yield
            for i in range(3):
                link(V.tensor_scalar(ws32[:, i, :], w32[:, i, :], omx[:, i:i + 1], SW, ALU.mult, ALU.mult))
                yield
                link(V.tensor_scalar(ws32[:, 3 + i, :], w32[:, i, :], mx[:, i:i + 1], SW, ALU.mult, ALU.mult))
                yield
            link(V.tensor_scalar(ws32[:, 6, :], w32[:, 3, :], SW, None, ALU.mult))
            yield
            link(V.tensor_copy(wph[:, :, :], ws32[:, :, :]))
            yield
            link(V.tensor_tensor(wpl[:, :, :], ws32[:, :, :], wph[:, :, :], ALU.subtract))
            yield
            link(V.tensor_scalar(brs[:, :], brk[:, :], SW, None, ALU.mult))
            yield
            wait(V, "bias_in", 32)
            link(V.tensor_scalar(bro[0:2, :], bro[0:2, :], SW, None, ALU.mult))
            yield
            link(V.tensor_copy(brh[0:2, :], bro[0:2, :]))
            yield
            link(V.tensor_tensor(brl[0:2, :], bro[0:2, :], brh[0:2, :], ALU.subtract))
            yield
            link(V.memset(brw[:, :], 0.0))
            yield
            link(V.tensor_scalar(bro[0:2, :], brh[0:2, :], C("ident")[0:2, 0:1], None, ALU.mult))
            yield
            link(V.scalar_tensor_tensor(brw[0:2, :], brl[0:2, :], C("ident")[0:2, 1:2], bro[0:2, :],
                                        ALU.mult, ALU.add))
            yield
            link(V.tensor_copy(f2[:, :], C("first2")))
            yield
            done(V.tensor_copy(f2y[:, :], C("first2y")), "aconst_ready")

        def pool_state0():
            wait(G, "w_hi", 3 * (EXPERTS + 1))
            wait(G, "w_lo", 3 * (EXPERTS + 1))
            done(G.memset(st[0], 0.0), "ready")

        def sp_bias():
            for i in range(2):
                done(nc.sync.dma_start(bro[i:i + 1, :], bias_rows), "bias_in", 16)

        def where(u):
            return u // NG, u % NG

        def cols(t, g, shift):
            def of(tt):
                v = t[:, 4 * g * XS:4 * (g + 1) * XS].rearrange("p (b s) -> p b s", s=XS)
                return v[:, :, 2 + tt * P - shift:2 + (tt + 1) * P - shift]
            return of

        PR, KV, PK, PO = 0, (1, 2), 3, 4
        proj_order = []

        def prow(u, k):
            return proj_order.index((u, k))

        def wait_left(eng, n):
            u, k = proj_order[n]
            if k in (PR, PK):
                wait(eng, "r32" if k == PR else "k32", u + 1)
            else:
                wait(eng, "proj_free", sum(kk not in (PR, PK) for _, kk in proj_order[:n + 1]))

        def pe_proj(u, k):
            tt, g = where(u)
            n = prow(u, k)
            o = psum[n % 2]
            if n >= 2:
                wait_left(T, n - 2)
            if u == 0 and k == 0:
                wait(T, "gated", 2 * NU - 1)
                wait(T, "zero_cols", 2 * nb)
                wait(T, "aconst_ready", 1)
            if k not in KV:
                i = 0
                for shift in range(2):
                    mh, ml = cols(xh, g, shift)(tt), cols(xl, g, shift)(tt)
                    wsl = 3 * shift + (k == PK)
                    for a, m in ((wph, mh), (wph, ml), (wpl, mh)):
                        j = T.matmul(o[:, :], a[:, wsl, :], m, start=(i == 0), stop=(i == 5))
                        i += 1
            else:
                for s in range(2):
                    b = 2 * KV.index(k) + s
                    oo = o[:, s * 256:(s + 1) * 256]
                    T.matmul(oo, f2[:, :], brw[:, 0:256], start=True, stop=False)
                    i = 0
                    for shift in range(2):
                        ch, cl = cols(xh, g, shift)(tt)[:, b, :], cols(xl, g, shift)(tt)[:, b, :]
                        for a, m in ((ch, wph), (ch, wpl), (cl, wph)):
                            j = T.matmul(oo, a, m[:, 3 * shift + 1:3 * shift + 3, :].rearrange("p a d -> p (a d)"),
                                         start=False, stop=(i == 5))
                            i += 1
            done(j, "proj")

        def act_proj(u, k):
            n, s = prow(u, k), u % 2
            o = psum[n % 2]
            wait(A, "proj", n + 1)
            wait(A, "down", NU)
            if u >= 2:
                wait(A, "local", 16 * (u - 1))
                wait(A, "inter", 4 * (u - 1))
                if k in KV:
                    wait(A, "av", 16 * (u - 1))
            if k in KV:
                i = KV.index(k)
                wait(A, "kdec", 2 * u + i + 1)
                v3 = o[:, :].rearrange("p (s c) -> p s c", s=2)
                done(A.copy(vh[:, s, 2 * i:2 * i + 2, :], v3[:, :, P:2 * P]), "v_hi")
                done(A.copy(v32[:, s, 2 * i:2 * i + 2, :], v3[:, :, P:2 * P]), "v32")
                done(A.copy(kth[:, s, 2 * i:2 * i + 2, :], kt[:, i, :, :]), "kt_hi")
            elif k == PR:
                if u >= 2:
                    wait(A, "r_lo", u - 1)
                done(A.activation(r32[:, s, :], o[:, :], ACT.Identity, bias=brs[:, 0:1]), "r32")
                wait(A, "r32", u + 1)
                done(A.copy(rh[:, s, :], r32[:, s, :]), "r_hi")
            else:
                done(A.activation(k32[:, s, :], o[:, :], ACT.Identity, bias=brs[:, 1:2]), "k32")

        def act_mask(u, q):
            s = u % 2
            done(A.mul(rm[:, s, q, :], r32[:, s, :], C("slot")[:, q:q + 1]), "rmask")

        def dve_proj1(u, k):
            n = prow(u, k)
            if k in KV:
                i = KV.index(k)
                wait(V, "proj", n + 1)
                if u >= 1:
                    wait(V, "kt_lo", 2 * u + i - 1)
                v3 = psum[n % 2][:, :].rearrange("p (s c) -> p s c", s=2)
                done(V.tensor_tensor(kt[:, i, :, :], v3[:, :, 0:P], rep_mid(wk[:, :], 2), ALU.mult), "kdec")

        def dve_proj2(u, k):
            n, s = prow(u, k), u % 2
            o = psum[n % 2]
            if k in KV:
                i = KV.index(k)
                b = slice(2 * i, 2 * i + 2)
                v3 = o[:, :].rearrange("p (s c) -> p s c", s=2)
                wait(V, "v_hi", 2 * u + i + 1)
                wait(V, "v32", 2 * u + i + 1)
                done(V.tensor_tensor(vl[:, s, b, :], v3[:, :, P:2 * P], vh[:, s, b, :], ALU.subtract),
                     "proj_free")
                wait(V, "kt_hi", 2 * u + i + 1)
                done(V.tensor_tensor(ktl[:, s, b, :], kt[:, i, :, :], kth[:, s, b, :], ALU.subtract),
                     "kt_lo")
            elif k == PR:
                wait(V, "r_hi", u + 1)
                done(V.tensor_tensor(rl[:, s, :], r32[:, s, :], rh[:, s, :], ALU.subtract), "r_lo")

        def of_step(j):
            return j // 4, j % 4, j // 4 % NG

        def last_step(j):
            u, c, _ = of_step(j)
            return j - 1 if c else 4 * (u - NG) + 3

        def version(j):
            u, c, _ = of_step(j)
            return (4 * where(u)[0] + c) % 2

        def pe_inter(j):
            u, c, g = of_step(j)
            if c == 0 and u >= 1:
                wait(T, "yint", u)
            wait(T, "state_lo", j + 1)
            wait(T, "r_lo", u + 1)
            for b in range(4):
                o = psum[7][:, b * P + c * Q:b * P + (c + 1) * Q]
                S = slice(b * P, (b + 1) * P)
                R = slice(b * P + c * Q, b * P + (c + 1) * Q)
                T.matmul(o, sh[:, j % 2, S], rh[:, u % 2, R], start=True, stop=False)
                T.matmul(o, sh[:, j % 2, S], rl[:, u % 2, R], start=False, stop=False)
                k = T.matmul(o, sl[:, j % 2, S], rh[:, u % 2, R], start=False, stop=True)
            done(k, "inter")

        def pe_update(j):
            u, c, g = of_step(j)
            wait(T, "kt_lo", 2 * u + 2)
            if j >= 1:
                wait(T, "um", j)
            R = slice(c * Q, (c + 1) * Q)
            for b in range(4):
                o = psum[6][:, b * P:(b + 1) * P]
                T.matmul(o, kth[R, u % 2, b, :], vh[R, u % 2, b, :], start=True, stop=False)
                T.matmul(o, kth[R, u % 2, b, :], vl[R, u % 2, b, :], start=False, stop=False)
                k = T.matmul(o, ktl[R, u % 2, b, :], vh[R, u % 2, b, :], start=False, stop=True)
            done(k, "upd")

        def dve_update(j):
            wait(V, "upd", j + 1)
            if j >= NUM:
                wait(V, "state", j - NUM + 1)
            done(V.tensor_tensor(um[:, j % NUM, :].rearrange("p (b d) -> p b d", b=4),
                                 psum[6][:, :].rearrange("p (b d) -> p b d", b=4),
                                 rep_mid(C("head"), 4), ALU.mult), "um")

        def dve_state(j):
            u, c, g = of_step(j)
            wait(V, "um", j + 1)
            wait(V, "ready", 1)
            if last_step(j) >= 0:
                wait(V, "state", last_step(j) + 1)
                wait(V, "state_lo", last_step(j) + 1)
            a = version(j)
            done(V.scalar_tensor_tensor(st[1 - a][:, g, :], st[a][:, g, :], ws[:, 0:1], um[:, j % NUM, :],
                                        ALU.mult, ALU.add), "state")

        def act_state(j):
            u, c, g = of_step(j)
            if last_step(j) >= 0:
                wait(A, "state", last_step(j) + 1)
            else:
                wait(A, "ready", 1)
            if j >= 2:
                wait(A, "inter", j - 1)
            done(A.copy(sh[:, j % 2, :], st[version(j)][:, g, :]), "state_hi")

        def pool_state(j):
            u, c, g = of_step(j)
            wait(G, "state_hi", j + 1)
            done(G.tensor_tensor(sl[:, j % 2, :], st[version(j)][:, g, :], sh[:, j % 2, :], ALU.subtract),
                 "state_lo")

        def pe_local_av(u, b):
            i, s = 4 * u + b, u % 2
            n, (vu, vb) = i - 1, divmod(i - 1, 4)
            vs = vu % 2
            for g in range(CH):
                if u < NA:
                    if g == 0:
                        wait(T, "rmask", 4 * (u + 1))
                        wait(T, "k32", u + 1)
                        if i >= 2:
                            wait(T, "a_dec", i - 1)
                    R = slice(g * Q, (g + 1) * Q)
                    wait(T, "local", 4 * i + g)
                    for c in range(CH):
                        X = slice(b * P + c * Q, b * P + (c + 1) * Q)
                        k = T.matmul(psum[2 + i % 2][c * Q:(c + 1) * Q, g * P:(g + 1) * P],
                                     k32[R, s, X], rm[R, s, :, X], start=True, stop=True)
                    done(k, "local")
                if n >= 0:
                    c = g
                    if c == 0:
                        wait(T, "a_dec", n + 1)
                        if n >= 2:
                            wait(T, "ysel", 3 * (n - 1))
                    R = slice(c * Q, (c + 1) * Q)
                    wait(T, "av", 4 * n + c)
                    for m in range(CH):
                        M, N = slice(m * Q, (m + 1) * Q), slice(m * P, (m + 1) * P)
                        k = T.matmul(psum[4 + n % 2][M, c * P:(c + 1) * P],
                                     v32[R, vs, vb, M], a32[R, n % 2, N], start=True, stop=True)
                    done(k, "av")

        def dve_local(u, b):
            i = 4 * u + b
            wait(V, "local", 4 * (i + 1))
            if i >= 2:
                wait(V, "av", 4 * (i - 1))
            done(V.tensor_tensor(a32[:, i % 2, :], psum[2 + i % 2][:, :],
                                 wmat[:, :, :].rearrange("p h i -> p (h i)"), ALU.mult), "a_dec")

        def act_av(u, b):
            i = 4 * u + b
            wait(A, "av", 4 * (i + 1))
            if u >= 2:
                wait(A, "y32", u - 1)
            y4 = psum[4 + i % 2][:, :].rearrange("p (c q i) -> p c q i", c=CH, q=HPG)
            done(A.mul(yacc[:, u % 2, b, :].rearrange("p (c i) -> p c i", c=CH), y4[:, :, 0, :],
                       C("slot_y")[:, 0:1]), "ysel0")

        def dve_av(u, b):
            i = 4 * u + b
            wait(V, "ysel0", i + 1)
            y4 = psum[4 + i % 2][:, :].rearrange("p (c q i) -> p c q i", c=CH, q=HPG)
            acc = yacc[:, u % 2, b, :].rearrange("p (c i) -> p c i", c=CH)
            for q in range(1, HPG):
                m = C("slot_y")[:, q:q + 1]
                if q > 1:
                    wait(V, "ysel", 3 * i + q - 1)
                done(V.scalar_tensor_tensor(acc, y4[:, :, q, :], m, acc, ALU.mult, ALU.add), "ysel")

        def dve_join1(u):
            s = u % 2
            wait(V, "inter", 4 * (u + 1))
            done(V.tensor_tensor(yint[:, s, :].rearrange("p (a i) -> p a i", i=Q),
                                 psum[7][:, :].rearrange("p (a i) -> p a i", i=Q),
                                 rep_mid(wb[:, :], 16), ALU.mult), "yint")

        def dve_join2(u):
            s = u % 2
            wait(V, "yint", u + 1)
            wait(V, "ysel", 12 * (u + 1))
            if u >= 2:
                wait(V, "y_lo", u - 1)
            done(V.tensor_tensor(y32[:, s, :], yint[:, s, :], yacc[:, s, :, :].rearrange("p b d -> p (b d)"),
                                 ALU.add), "y32")

        def act_join(u):
            s = u % 2
            wait(A, "y32", u + 1)
            if u >= 2:
                wait(A, "proj", prow(u - 2, PO) + 1)
            done(A.copy(yh[:, s, :], y32[:, s, :]), "y_hi")

        def dve_join3(u):
            s = u % 2
            wait(V, "y_hi", u + 1)
            done(V.tensor_tensor(yl[:, s, :], y32[:, s, :], yh[:, s, :], ALU.subtract), "y_lo")

        def pe_out(u):
            s, n = u % 2, prow(u, PO)
            wait(T, "y_lo", u + 1)
            wait_left(T, n - 2)
            for b in range(4):
                o = psum[n % 2][:, b * P:(b + 1) * P]
                D = slice(b * P, (b + 1) * P)
                T.matmul(o, f2y[:, :], brw[:, 2 * P:3 * P], start=True, stop=False)
                T.matmul(o, yh[:, s, D], wph[:, 6, :], start=False, stop=False)
                T.matmul(o, yh[:, s, D], wpl[:, 6, :], start=False, stop=False)
                k = T.matmul(o, yl[:, s, D], wph[:, 6, :], start=False, stop=True)
            done(k, "proj")

        def tile(u, b):
            tt, g = where(u)
            return (4 * g + b) * TPS + tt

        def sp_fetch(u):
            tt, g = where(u)
            wait(nc.sync, "down", NU)
            if u >= 2:
                wait(nc.sync, "res", u - 1)
            done(nc.sync.dma_start(xin[:, u % 2, :, :], x_unit[g, tt]), f"x_again{u % 2}", 16)

        def pool_fetch(u, b):
            if u == 0 and b == 0:
                wait(G, "down", NU)
                for i in range(NYB):
                    wait(G, f"y_stored{i}", 16 * len(range(i, ROUTED, NYB)))
            if u >= 2:
                wait(G, "moe", 4 * (u - 1))
            t = tile(u, b)
            for k in range(2):
                done(G.indirect_dma_start(picked[k][:, u % 2, b, :], None, rows_out,
                                          bass.IndirectOffsetOnAxis(pos[k][:, t:t + 1], 0)),
                     f"picked{u % 2}", 16)

        def pool_moe(u, part):
            s = u % 2
            tt, g = where(u)

            def of_unit(a):
                v = a[:, 4 * g * TPS:4 * (g + 1) * TPS]
                if len(a.shape) == 2:
                    return v.rearrange("p (b t) -> p b t", t=TPS)[:, :, tt]
                return v.rearrange("p (b t) d -> p b t d", t=TPS)[:, :, tt, :]

            p0, p1, m = picked[0][:, s, :, :], picked[1][:, s, :, :], mo[:, s, :, :]
            if part == 0:
                wait(G, f"picked{s}", 16 * 8 * (u // 2 + 1))
                wait(G, "y_out", SHARED)
                wait(G, "gates", 2)
                i = G.tensor_tensor(p0, p0, rep(of_unit(gates[0]), P), ALU.mult)
            elif part == 1:
                i = G.tensor_tensor(p1, p1, rep(of_unit(gates[1]), P), ALU.mult)
            elif part == 2:
                if u >= 2:
                    wait(G, "moe_silu", u - 1)
                wait(G, "moe", 4 * u + 1)
                i = G.tensor_tensor(m, p0, of_unit(ffn), ALU.add)
            else:
                wait(G, "moe", 4 * u + 3)
                i = G.tensor_tensor(m, m, p1, ALU.add)
            done(i, "moe")

        def act_moe(u):
            s = u % 2
            wait(A, "moe", 4 * (u + 1))
            if u >= 2:
                wait(A, "res", u - 1)
            done(A.activation(gt[:, s, :], mo[:, s, :, :].rearrange("p b d -> p (b d)"), ACT.Silu), "moe_silu")

        def dve_end(u):
            s, n = u % 2, prow(u, PO)
            wait(V, "proj", n + 1)
            wait(V, "moe_silu", u + 1)
            if u >= 2:
                wait(V, f"stored{s}", 16 * (u // 2))
            done(V.scalar_tensor_tensor(res[:, s, :], psum[n % 2][:, :], 1.0 / SY / SW, gt[:, s, :],
                                        ALU.mult, ALU.mult), "proj_free")
            wait_left(V, n)
            wait(V, f"x_again{s}", 16 * (u // 2 + 1))
            done(V.tensor_tensor(res[:, s, :], res[:, s, :], xin[:, s, :, :].rearrange("p b d -> p (b d)"),
                                 ALU.add), "res")

        def sp_end(u):
            tt, g = where(u)
            wait(nc.sync, "res", u + 1)
            done(nc.sync.dma_start(out_unit[g, tt], res[:, u % 2, :].rearrange("p (b d) -> p b d", b=4)),
                 f"stored{u % 2}", 16)

        stages = {
            "start": dict(sp=sp_start, dve=dve_prologue, pool=pool_prologue),
            "bias": dict(sp=sp_bias),
            "weights_in": dict(sp=sp_weights),
            "zero": dict(sp=sp_zero),
            "stats": dict(dve=dve_stats, act=act_std),
            "norm": dict(dve=dve_norm, act=act_norm, pool=pool_norm),
            "flip": dict(pe=pe_flip, act=act_flip),
            "flip2": dict(dve=dve_flip),
            "gate": dict(pe=pe_gate),
            "split_w": dict(act=act_split_w, dve=dve_split_w),
            "route": dict(dve=lambda n: dve_steps(route_steps, n)),
            "count": dict(pe=pe_route),
            "exps": dict(act=act_route),
            "scatter": dict(pool=pool_scatter),
            "aconst": dict(dve=lambda n: dve_steps(aconst_steps, n)),
            "rates": dict(act=act_rates),
            "decays": dict(act=act_decays),
            "sorted_in": dict(sp=sp_sorted),
            "sorted": dict(pe=pe_sorted, act=act_sorted, dve=dve_sorted),
            "up": dict(pe=pe_up, act=act_up, dve=dve_up),
            "split": dict(act=act_split, dve=dve_split),
            "down": dict(pe=pe_down, act=act_down, sp=sp_down),
            "state0": dict(pool=pool_state0),
            "proj": dict(pe=pe_proj, act=act_proj, dve=dve_proj1),
            "proj_products": dict(pe=pe_proj),
            "proj_rest": dict(act=act_proj, dve=dve_proj1),
            "proj2": dict(dve=dve_proj2),
            "mask": dict(act=act_mask),
            "inter": dict(pe=pe_inter),
            "update": dict(pe=pe_update),
            "own_blocks": dict(dve=dve_update),
            "state": dict(dve=dve_state),
            "state_parts": dict(act=act_state, pool=pool_state),
            "products": dict(pe=pe_local_av),
            "local": dict(dve=dve_local),
            "av": dict(act=act_av, dve=dve_av),
            "join_state": dict(dve=dve_join1),
            "join": dict(dve=dve_join2, act=act_join),
            "join2": dict(dve=dve_join3),
            "out": dict(pe=pe_out),
            "x_again": dict(sp=sp_fetch),
            "fetch": dict(pool=pool_fetch),
            "moe": dict(pool=pool_moe),
            "gating": dict(act=act_moe),
            "end": dict(dve=dve_end, sp=sp_end),
        }
        plan = [("start",), ("bias",), ("weights_in", 0), ("weights_in", 1), ("zero",)]
        for b in range(nb + 3):
            if b < nb:
                plan.append(("stats", b))
            if 1 <= b <= nb:
                plan.append(("norm", b - 1))
            if 2 <= b < nb + 2:
                plan.append(("flip", b - 2))
            if b >= 3:
                plan += [("flip2", b - 3), ("gate", b - 3)]
            if b == nb // 2:
                plan += [("split_w", 0, part) for part in range(3)] + [("weights_in", 2)]
        plan += [("rates",), ("route", ROUTE_CHOSEN + 1), ("aconst", 1), ("count",), ("exps",), ("decays",)]
        plan += [("route", ROUTE_PLACES), ("scatter",)]
        split = 3
        for v in range(NU + 1):
            if v < NU:
                if routed(v):
                    first = v == SHARED
                    plan += [("sorted_in", w) for w in range(v if first else v + 2, min(v + 3, NU))]
                    if first:
                        plan.append(("sorted", v))
                for h in range(2):
                    plan.append(("up", v, h))
                    if h == 0 and routed(v) and v + 1 < NU:
                        plan.append(("sorted", v + 1))
                    if v < 2:
                        plan.append(("route", 3))
                    elif v >= 3 and (2 * v + h) % 3 != 2 and split < 3 * (EXPERTS + 1):
                        k, part = divmod(split, 3)
                        plan.append(("split_w", k, part))
                        if part == 2 and k + 2 <= EXPERTS:
                            plan.append(("weights_in", k + 2))
                        split += 1
                    if 3 <= v < SHARED:
                        plan.append(("aconst", 2))
                    plan.append(("split", v, h))
            if v > 0:
                plan.append(("down", v - 1))
        assert split == 3 * (EXPERTS + 1)

        def proj(u, k):
            proj_order.append((u, k))
            return ("proj", u, k)

        plan.insert(-1, ("proj_products",) + proj(0, 0)[1:])
        plan += [("state0",), ("x_again", 0)]
        plan += [("fetch", 0, b) for b in range(4)]
        for k in range(4):
            plan += [proj(0, k) if k else ("proj_rest", 0, k), ("proj2", 0, k), ("mask", 0, k)]
        plan += [("state_parts", 0), ("update", 0), ("own_blocks", 0), ("update", 1), ("own_blocks", 1)]
        NJ = 4 * NA
        for u in range(NA + 1):
            for i in range(4 if u < NA else 3):
                j = 4 * u + i
                now, more = u < NA, u + 1 < NA
                if now:
                    plan += [("inter", j), ("state", j)]
                    if i == 3:
                        plan.append(("join_state", u))
                    if j + 1 < NJ:
                        plan.append(("state_parts", j + 1))
                    plan.append(("moe", u, i))
                if more:
                    plan += [proj(u + 1, i), ("fetch", u + 1, i)]
                    if i == 0:
                        plan.append(("x_again", u + 1))
                if i == 2 and u > 0:
                    proj_order.append((u - 1, PO))
                    plan.append(("out", u - 1))
                if now and j + 2 < NJ and i not in (0, 2):
                    plan.append(("update", j + 2))
                if now or i == 0:
                    plan.append(("products", u, i))
                if now and j + 2 < NJ and i in (0, 2):
                    plan.append(("update", j + 2))
                if more:
                    plan += [("proj2", u + 1, i), ("mask", u + 1, i)]
                if now:
                    plan.append(("local", u, i))
                if i == 2 and u > 0:
                    plan.append(("end", u - 1))
                if now and j + 2 < NJ:
                    plan.append(("own_blocks", j + 2))
                last = (u, i - 1) if i else (u - 1, 3)
                if 0 <= last[0] < NA:
                    plan.append(("av", *last))
                if i == 0 and u > 0:
                    plan += [("join", u - 1), ("gating", u - 1)]
                if i == 1 and u > 0:
                    plan.append(("join2", u - 1))

        def run(kind):
            for name, *args in plan:
                if kind in stages[name]:
                    stages[name][kind](*args)

        @block.sync
        def _(e):
            run("sp")
            for s in range(2):
                e.wait_ge(sem(f"stored{s}"), 16 * len(range(s, NA, 2)))

        @block.gpsimd
        def _(e):
            run("pool")

        @block.scalar
        def _(e):
            run("act")

        @block.vector
        def _(e):
            run("dve")

        @block.tensor
        def _(e):
            run("pe")


def kernel(**inputs):
    import concourse.bacc as bacc
    from concourse.bass_utils import run_bass_kernel_spmd

    a = {k[3:]: np.asarray(v) for k, v in inputs.items()}
    x = np.ascontiguousarray(a["attn_x"])
    nb = x.shape[0]
    arrays = {
        "x": x,
        "decay": np.repeat(a["attn_time_decay"], HD)[:, None],
        "per_head": np.broadcast_to(np.concatenate([a["attn_time_decay"], a["attn_time_faaaa"]]), (P, 2 * HEADS)),
        "maa": np.stack([a["attn_time_maa_r"], a["attn_time_maa_k"], a["attn_time_maa_v"]], 1),
        "wT": np.stack([a["attn_Wr"].T, a["attn_Wk"].T, a["attn_Wv"].T, a["attn_Wo"].T], 1),
        "bias": np.stack([a["attn_br"], a["attn_bk"]], 1),
        "bias_rows": np.concatenate([a["attn_bk"], a["attn_bv"], a["attn_bo"]])[None, :],
        "gateT": a["ffn_gate_W"].T,
        "w1e": a["ffn_w1_e"], "w3e": a["ffn_w3_e"], "w2e": a["ffn_w2_e"],
        "w1s": a["ffn_w1_s"], "w3s": a["ffn_w3_s"], "w2s": a["ffn_w2_s"],
        "const": constants(2 * nb * SEQ // UNIT + EXPERTS - 1),
    }
    arrays = {k: np.ascontiguousarray(v) for k, v in arrays.items()}
    nc = bacc.Bacc("TRN2", target_bir_lowering=False, num_devices=1)
    aps = {k: nc.dram_tensor(k, v.shape, mybir.dt.from_np(v.dtype), kind="ExternalInput").ap()
           for k, v in arrays.items()}
    out = nc.dram_tensor("out", x.shape, F32, kind="ExternalOutput").ap()
    build(nc, nb, *[aps[k] for k in arrays], out)
    return run_bass_kernel_spmd(nc, [arrays], core_ids=[0]).results[0]["out"]
```
